# Optimizing a Trainium2 kernel written in Bass

```python
import numpy as np
import jax
import jax.numpy as jnp

def _softmax(x, axis=-1):
    return jax.nn.softmax(x, axis=axis)

def _gelu(x):
    return jax.nn.gelu(x, approximate=True)

def _silu(x):
    return jax.nn.silu(x)

def _sigmoid(x):
    return jax.nn.sigmoid(x)

def _layernorm(x, axis=-1, eps=1e-05):
    m = jnp.mean(x, axis=axis, keepdims=True)
    v = jnp.var(x, axis=axis, keepdims=True)
    return (x - m) / jnp.sqrt(v + eps)

def _scatter_add(tgt, idx, src, axis=0):
    return tgt.at[idx].add(src)

def _segment_sum(src, seg, n):
    return jax.ops.segment_sum(src, seg, n)
kernel_name = 'mk_vit_tower_d1_tok_img768_r4_3629e8'

def setup_inputs(seed: int=0):
    np.random.seed(seed)
    _w = jnp.asarray

    def _rec_inputs():
        import jax
        import jax.numpy as jnp
        _rk = jax.random.key(seed)
        x = -0.000222058 + 0.999998 * jax.random.normal(jax.random.fold_in(_rk, 1), (8, 3, 128, 128), jnp.float32)
        return x
    x = _rec_inputs()

    def _L0_tok_setup():
        import jax, jax.numpy as jnp
        import numpy as np
        PATCH = 16

        def _patchify(x, patch):
            b, c, H, W = x.shape
            ph_pad, pw_pad = (H % patch, W % patch)
            x = jnp.pad(x, ((0, 0), (0, 0), (ph_pad, 0), (pw_pad, 0)))
            H2, W2 = (H + ph_pad, W + pw_pad)
            nh, nw = (H2 // patch, W2 // patch)
            x = x.reshape(b, c, nh, patch, nw, patch)
            x = x.transpose(0, 2, 4, 3, 5, 1)
            return x.reshape(b, nh * nw, patch * patch * c)
        key = jax.random.key(seed)
        k1, k2, k3 = jax.random.split(key, 3)
        d_model, c = (192, 3)
        in_feat = PATCH * PATCH * c
        x = jax.random.normal(k1, (32, c, 128, 128), dtype=jnp.float32)
        W = jax.random.normal(k2, (d_model, in_feat), dtype=jnp.float32) * (1.0 / np.sqrt(in_feat))
        b = jax.random.normal(k3, (d_model,), dtype=jnp.float32) * 0.01
        return {'x': x, 'W': W, 'b': b}
    _L0_tok_all = _L0_tok_setup()
    _L0_tok_in = {k: v for k, v in _L0_tok_all.items() if k in ('W', 'b')}
    del _L0_tok_all

    def _L0_attn_setup():
        import jax, jax.numpy as jnp
        import numpy as np
        B, L, D, H = (2, 512, 192, 12)
        HD = D // H
        ROPE_BASE = 10000.0

        def apply_rope(x):
            d = x.shape[-1]
            pos = jnp.arange(x.shape[2], dtype=jnp.float32)
            inv_freq = 1.0 / ROPE_BASE ** (jnp.arange(0, d, 2, dtype=jnp.float32) / d)
            ang = pos[:, None] * inv_freq[None, :]
            cos = jnp.concatenate([jnp.cos(ang), jnp.cos(ang)], axis=-1)
            sin = jnp.concatenate([jnp.sin(ang), jnp.sin(ang)], axis=-1)
            x1, x2 = jnp.split(x, 2, axis=-1)
            rot = jnp.concatenate([-x2, x1], axis=-1)
            return x * cos[None, None, :, :].astype(x.dtype) + rot * sin[None, None, :, :].astype(x.dtype)
        key = jax.random.key(seed)
        ks = jax.random.split(key, 9)
        s = 1.0 / np.sqrt(D)
        return {'query': jax.random.normal(ks[0], (B, L, D), dtype=jnp.float32), 'Wq': jax.random.uniform(ks[1], (D, D), jnp.float32, -s, s), 'bq': jax.random.uniform(ks[2], (D,), jnp.float32, -s, s), 'Wk': jax.random.uniform(ks[3], (D, D), jnp.float32, -s, s), 'bk': jax.random.uniform(ks[4], (D,), jnp.float32, -s, s), 'Wv': jax.random.uniform(ks[5], (D, D), jnp.float32, -s, s), 'bv': jax.random.uniform(ks[6], (D,), jnp.float32, -s, s), 'Wo': jax.random.uniform(ks[7], (D, D), jnp.float32, -s, s), 'bo': jax.random.uniform(ks[8], (D,), jnp.float32, -s, s)}
    _L0_attn_all = _L0_attn_setup()
    _L0_attn_in = {k: v for k, v in _L0_attn_all.items() if k in ('Wq', 'bq', 'Wk', 'bk', 'Wv', 'bv', 'Wo', 'bo')}
    del _L0_attn_all

    def _L0_ffn_setup():
        import jax, jax.numpy as jnp
        import numpy as np
        E, TOPK = (32, 2)
        D, HID, BOT, OUT = (192, 512, 64, 192)
        B, S = (2, 128)
        key = jax.random.key(seed)
        ks = jax.random.split(key, 7)
        p = lambda k, shape: jax.random.normal(k, shape, dtype=jnp.float32) * 0.02
        return {'x': jax.random.normal(ks[0], (B, S, D), dtype=jnp.float32), 'gate_w': p(ks[1], (E, D)), 'W1': p(ks[2], (E, D, HID)), 'b1': jnp.zeros((E, HID), jnp.float32), 'W2': p(ks[3], (E, HID, HID)), 'b2': jnp.zeros((E, HID), jnp.float32), 'W3': p(ks[4], (E, HID, BOT)), 'b3': jnp.zeros((E, BOT), jnp.float32), 'Wl': p(ks[5], (E, BOT, OUT)), 'bl': jnp.zeros((E, OUT), jnp.float32)}
    _L0_ffn_all = _L0_ffn_setup()
    _L0_ffn_in = {k: v for k, v in _L0_ffn_all.items() if k in ('gate_w', 'W1', 'b1', 'W2', 'b2', 'W3', 'b3', 'Wl', 'bl')}
    del _L0_ffn_all
    return {'x': x, 'L0_tok_W': _L0_tok_in['W'], 'L0_tok_b': _L0_tok_in['b'], 'L0_attn_Wq': _L0_attn_in['Wq'], 'L0_attn_bq': _L0_attn_in['bq'], 'L0_attn_Wk': _L0_attn_in['Wk'], 'L0_attn_bk': _L0_attn_in['bk'], 'L0_attn_Wv': _L0_attn_in['Wv'], 'L0_attn_bv': _L0_attn_in['bv'], 'L0_attn_Wo': _L0_attn_in['Wo'], 'L0_attn_bo': _L0_attn_in['bo'], 'L0_ffn_gate_w': _L0_ffn_in['gate_w'], 'L0_ffn_W1': _L0_ffn_in['W1'], 'L0_ffn_b1': _L0_ffn_in['b1'], 'L0_ffn_W2': _L0_ffn_in['W2'], 'L0_ffn_b2': _L0_ffn_in['b2'], 'L0_ffn_W3': _L0_ffn_in['W3'], 'L0_ffn_b3': _L0_ffn_in['b3'], 'L0_ffn_Wl': _L0_ffn_in['Wl'], 'L0_ffn_bl': _L0_ffn_in['bl']}

def reference(x, L0_tok_W, L0_tok_b, L0_attn_Wq, L0_attn_bq, L0_attn_Wk, L0_attn_bk, L0_attn_Wv, L0_attn_bv, L0_attn_Wo, L0_attn_bo, L0_ffn_gate_w, L0_ffn_W1, L0_ffn_b1, L0_ffn_W2, L0_ffn_b2, L0_ffn_W3, L0_ffn_b3, L0_ffn_Wl, L0_ffn_bl):
    import jax
    import jax.numpy as jnp

    def _L0_tok_ref(x, W, b):
        import jax, jax.numpy as jnp
        import numpy as np
        PATCH = 16

        def _patchify(x, patch):
            b, c, H, W = x.shape
            ph_pad, pw_pad = (H % patch, W % patch)
            x = jnp.pad(x, ((0, 0), (0, 0), (ph_pad, 0), (pw_pad, 0)))
            H2, W2 = (H + ph_pad, W + pw_pad)
            nh, nw = (H2 // patch, W2 // patch)
            x = x.reshape(b, c, nh, patch, nw, patch)
            x = x.transpose(0, 2, 4, 3, 5, 1)
            return x.reshape(b, nh * nw, patch * patch * c)
        patches = _patchify(x, PATCH)
        return jnp.einsum('bnf,df->bnd', patches, W) + b

    def _L0_attn_ref(query, Wq, bq, Wk, bk, Wv, bv, Wo, bo):
        import jax, jax.numpy as jnp
        import numpy as np
        B, L, D, H = (2, 512, 192, 12)
        HD = D // H
        ROPE_BASE = 10000.0

        def apply_rope(x):
            d = x.shape[-1]
            pos = jnp.arange(x.shape[2], dtype=jnp.float32)
            inv_freq = 1.0 / ROPE_BASE ** (jnp.arange(0, d, 2, dtype=jnp.float32) / d)
            ang = pos[:, None] * inv_freq[None, :]
            cos = jnp.concatenate([jnp.cos(ang), jnp.cos(ang)], axis=-1)
            sin = jnp.concatenate([jnp.sin(ang), jnp.sin(ang)], axis=-1)
            x1, x2 = jnp.split(x, 2, axis=-1)
            rot = jnp.concatenate([-x2, x1], axis=-1)
            return x * cos[None, None, :, :].astype(x.dtype) + rot * sin[None, None, :, :].astype(x.dtype)
        b, l, _ = query.shape
        q = (query @ Wq.T + bq).reshape(b, l, H, HD).transpose(0, 2, 1, 3)
        k = (query @ Wk.T + bk).reshape(b, l, H, HD).transpose(0, 2, 1, 3)
        v = (query @ Wv.T + bv).reshape(b, l, H, HD).transpose(0, 2, 1, 3)
        q = apply_rope(q)
        k = apply_rope(k)
        scores = jnp.einsum('bhqd,bhkd->bhqk', q, k) / np.sqrt(HD).astype(np.float32)
        causal = jnp.triu(jnp.ones((l, l), dtype=bool), k=1)
        scores = jnp.where(causal[None, None, :, :], -jnp.inf, scores)
        attn = jax.nn.softmax(scores, axis=-1)
        out = jnp.einsum('bhqk,bhkd->bhqd', attn, v)
        out = out.transpose(0, 2, 1, 3).reshape(b, l, D)
        return out @ Wo.T + bo

    def _L0_ffn_ref(x, gate_w, W1, b1, W2, b2, W3, b3, Wl, bl):
        import jax, jax.numpy as jnp
        import numpy as np
        E, TOPK = (32, 2)
        D, HID, BOT, OUT = (192, 512, 64, 192)
        B, S = (2, 128)
        Bz, Sl, d = x.shape
        xt = x.reshape(-1, d)
        scores = jax.nn.softmax(xt @ gate_w.T, axis=-1)
        topk_w, topk_idx = jax.lax.top_k(scores, TOPK)
        topk_w = topk_w / (topk_w.sum(-1, keepdims=True) + 1e-20)
        gelu = lambda v: jax.nn.gelu(v, approximate=False)
        h = gelu(jnp.einsum('nd,edh->enh', xt, W1) + b1[:, None, :])
        h = gelu(jnp.einsum('enh,ehg->eng', h, W2) + b2[:, None, :])
        z = jnp.einsum('eng,egb->enb', h, W3) + b3[:, None, :]
        out_all = jnp.einsum('enb,ebo->eno', z, Wl) + bl[:, None, :]
        sel = jnp.take_along_axis(out_all.transpose(1, 0, 2), topk_idx[:, :, None], axis=1)
        y = (sel * topk_w[:, :, None]).sum(axis=1)
        return y.reshape(Bz, Sl, OUT)
    h = _L0_tok_ref(x, L0_tok_W, L0_tok_b)
    h = h + _L0_attn_ref(_layernorm(h, axis=-1), L0_attn_Wq, L0_attn_bq, L0_attn_Wk, L0_attn_bk, L0_attn_Wv, L0_attn_bv, L0_attn_Wo, L0_attn_bo)
    h = h + _L0_ffn_ref(_layernorm(h, axis=-1), L0_ffn_gate_w, L0_ffn_W1, L0_ffn_b1, L0_ffn_W2, L0_ffn_b2, L0_ffn_W3, L0_ffn_b3, L0_ffn_Wl, L0_ffn_bl)
    return h

_drawn_inputs = setup_inputs


def setup_inputs(seed=0):
    import zlib

    import numpy as np

    out = dict(_drawn_inputs(seed))
    spreads = {'L0_ffn_b1': (0.0, 0.8),
     'L0_ffn_b2': (0.0, 0.8),
     'L0_ffn_b3': (0.0, 0.722),
     'L0_ffn_bl': (0.0, 0.8)}
    factors = {'L0_tok_b': 4.27,
     'L0_attn_bq': 8.0,
     'L0_attn_bk': 8.0,
     'L0_ffn_W1': 8.0,
     'L0_ffn_W2': 8.0,
     'L0_ffn_W3': 8.0,
     'L0_ffn_Wl': 4.85}
    for name, (base, spread) in spreads.items():
        noise = np.random.default_rng([zlib.crc32(name.encode()), seed]).standard_normal(out[name].shape)
        drawn = base * np.exp(spread * noise) if base else spread * noise
        out[name] = jnp.asarray(drawn.astype(out[name].dtype))
    for name, factor in factors.items():
        out[name] = (out[name] * factor).astype(out[name].dtype)
    return out
```

```python
from contextlib import ExitStack

import concourse.bass as bass
from concourse import mybir

F32 = mybir.dt.float32
BF16 = mybir.dt.bfloat16
I32 = mybir.dt.int32
U32 = mybir.dt.uint32
ALU = mybir.AluOpType
ACT = mybir.ActivationFunctionType
AX = mybir.AxisListType

P = 128
TOKENS, D = 512, 192
TILES = TOKENS // P
SEQ = 64
FEAT = 768
KT = FEAT // P
HEADS, HD = 12, 16
D0, D1 = 128, 64
H0, H1 = D0 // HD, D1 // HD
HP = HEADS // 2
VC = 2 * (HD + 1)
E, HID, BOT = 32, 512, 64
HT = HID // P
UNITS = E // 2
CAP = 64
EXTRA = 2 * TOKENS // CAP
ROW = D + 2
RING = 4
W1C, W2C, W3C = 3 * HID, 2 * HT * HID, 2 * HT * BOT
LO, HI = W1C, W2C + W3C + D
WC = LO + HI
EPS = 1e-5

C_ID, C_TRI, C_CAUS, C_COS, C_SIN, C_M0, C_M1, C_IOTA, C_OFFA, C_OFFB, C_TOK, C_PAIR = range(12)
C_COLS = [P, P, SEQ, 2 * HD, 2 * HD, H0, H1, E, 1, 1, TILES + 1, UNITS]
C_AT = [sum(C_COLS[:i]) for i in range(len(C_COLS) + 1)]
NC_ = C_AT[-1]


def vit_layer(nc, xp_d, wt_d, wqk_d, wv_d, wo_d, gate_d, rows_d, bv_d, consts_d, experts_d,
              b12_d, b3_d, bl_d, out_d):
    slots_d = nc.dram_tensor("slots_d", ((UNITS + EXTRA) * P, ROW), F32, kind="Internal").ap()
    sums_d = nc.dram_tensor("sums_d", (TOKENS + P, D), F32, kind="Internal").ap()
    ctx = ExitStack()
    with ctx:
        def sb(name, shape, dt=F32):
            return ctx.enter_context(nc.sbuf_tensor(name, shape, dt))

        def sem(name):
            return ctx.enter_context(nc.semaphore(name))

        ring = sb("ring", [P, RING, WC])
        cst = sb("cst", [P, NC_])

        def const(i):
            return cst[:, C_AT[i]:C_AT[i + 1]]
        ident = const(C_ID)
        xp = sb("xp", [P, TILES, KT * P])
        wt = sb("wt", [P, KT, D])
        wqk0, wqk1 = sb("wqk0", [P, 2 * D]), sb("wqk1", [D1, 2 * D])
        wv0, wv1 = sb("wv0", [P, D]), sb("wv1", [D1, D])
        wo0, wo1 = sb("wo0", [P, D]), sb("wo1", [D1, D])
        g0, g1 = sb("g0", [P, E]), sb("g1", [D1, E])
        rows = sb("rows", [P, 4 * D])
        bv = sb("bv", [P, HP * HD])
        b12 = sb("b12", [P, UNITS, 2, HT * 2])
        b3 = sb("b3", [P, UNITS])
        bl = sb("bl", [E, D])
        identb = sb("identb", [P, P], BF16)
        causb = sb("causb", [P, H0, SEQ], BF16)
        trib = sb("trib", [P, P], BF16)
        onesb = sb("onesb", [P, P], BF16)
        halfneg = sb("halfneg", [P, 1])

        h = sb("h", [P, TILES, D])
        stats = sb("stats", [P, TILES, 6])
        mv = sb("mv", [P, TILES, 2])
        rstd = sb("rstd", [P, TILES])
        xn = sb("xn", [P, 2, D])
        xnT = sb("xnT", [P, 2, 2, P])
        qkb = sb("qkb", [P, 2, 2 * D])
        rcos = sb("rcos", [P, 2, 2 * D])
        rsin = sb("rsin", [P, 2 * D])
        rot = sb("rot", [P, 2, 2 * D])
        qT = sb("qT", [P, 2, 2, P])
        kx0 = sb("kx0", [P, 2, 2, H0 * SEQ])
        kx1 = sb("kx1", [P, 2, 2, H1 * SEQ])
        vbd = sb("vbd", [P, TILES, 2, HP * VC])
        smax = sb("smax", [P, 2, HEADS])
        ssub = sb("ssub", [P, HEADS * SEQ])
        prob = sb("prob", [P, 2, HEADS * SEQ])
        pT = sb("pT", [P, 2, HP * P])
        rden = sb("rden", [P, 2, HEADS])
        att = sb("att", [P, 2, D])
        attT = sb("attT", [P, 2, 2, P])
        h2 = sb("h2", [P, TILES, D])
        row1 = sb("row1", [P, TILES, ROW])
        row2 = sb("row2", [P, TILES, ROW])
        xn2T = sb("xn2T", [P, 2, 2, P])
        lg = sb("lg", [P, TILES, E])
        gs = sb("gs", [P, TILES, E])
        ge = sb("ge", [P, TILES, E])
        prb = sb("prb", [P, TILES, E])
        s4 = sb("s4", [P, 8, TILES])
        top = sb("top", [P, TILES, 8])
        topi = sb("topi", [P, TILES, 8], U32)
        topf = sb("topf", [P, TILES, 2])
        oh1, oh2 = sb("oh1", [P, TILES, E]), sb("oh2", [P, TILES, E])
        ohb = sb("ohb", [P, TILES, E], BF16)
        ranki = sb("ranki", [P, TILES, E], I32)
        rtmp = kx0[:].rearrange("p a i n -> p (a i n)")[:, 0:6 * TILES * E].rearrange("p (n c) -> p n c", n=6)
        sl1, sl2 = sb("sl1", [P, TILES], I32), sb("sl2", [P, TILES], I32)
        cnt = sb("cnt", [P, E])
        cnti = sb("cnti", [P, E], I32)
        xtra = sb("xtra", [P, 6, UNITS])
        bext = sb("bext", [P, E])
        xcount = sb("xcount", [1, EXTRA])
        xlist = sb("xlist", [1, EXTRA + 1], I32)
        wd = sb("wd", [P, TILES, E])
        y0 = prob[:, 0, :].rearrange("p (t d) -> p t d", t=TILES)
        wdT = prob[0:E, 1, 0:TILES * P].rearrange("p (t n) -> p t n", t=TILES)
        xtab = prob[0:1, 1, TILES * P:TILES * P + EXTRA * UNITS].rearrange("p (j u) -> p j u", j=EXTRA)
        blank = sb("blank", [P, ROW])

        xs = kx1[:].rearrange("p a i n -> p (a i n)")[:, 0:RING * ROW].rearrange("p (s c) -> p s c", s=RING)
        after_wt = wt[:].rearrange("p k d -> p (k d)")
        xm = after_wt[:, 0:2 * P].rearrange("p (b s) -> p b s", b=2)
        ob = after_wt[:, 2 * P:2 * P + 2 * D].rearrange("p (b d) -> p b d", b=2)
        xt = sb("xt", [P, 2, P])
        pre1, pre2, hb1, hb2, h1T_, h2T_ = (
            xp[:].rearrange("p t k -> p (t k)")[:, i * HID:(i + 1) * HID] for i in range(6))
        h1T, h2T = (v.rearrange("p (k s) -> p k s", k=HT) for v in (h1T_, h2T_))
        zbd = sb("zbd", [P, P])
        held = sb("held", [1, 1])
        ixa, ixb = sb("ixa", [P, 2], I32), sb("ixb", [P, 2], I32)

        bank = [ctx.enter_context(nc.psum_tensor(f"bank{i}", [P, 512], F32)) for i in range(8)]

        s_xp = [sem(f"s_xp{t}") for t in range(TILES)]
        s_wt, s_cst, s_rows, s_wqkv, s_late = map(sem, ("s_wt", "s_cst", "s_rows", "s_wqkv", "s_late"))
        s_lo = [sem(f"s_lo{i}") for i in range(RING)]
        s_hi = [sem(f"s_hi{i}") for i in range(RING)]
        s_set = sem("s_set")
        s_cast = sem("s_cast")
        s_v = sem("s_v")
        s_blank, s_scat, s_add, s_out = map(sem, ("s_blank", "s_scat", "s_add", "s_out"))
        s_xs = [sem(f"s_xs{i}") for i in range(RING)]
        (embedded, h_done, st1, rs1, xn_done, xnt_ps, xnt_done, qk_ps, v_ps, qkb_done, cos_done, v_done,
         rot_done, qt_ps, kt_ps, qt_done, kx1_done, kx0_done, sc_ps, sub_done, exp_done, pt_ps, pt_done,
         pv_ps, att_done, at_ps, at_done, wo_ps, hbo_done, st2, rs2, xn2_done, row2_done, x2_ps, x2_done,
         lg_ps, lg_done) = (sem(n) for n in (
             "embedded h_done st1 rs1 xn_done xnt_ps xnt_done qk_ps v_ps qkb_done cos_done v_done "
             "rot_done qt_ps kt_ps qt_done kx1_done kx0_done sc_ps sub_done exp_done pt_ps pt_done "
             "pv_ps att_done at_ps at_done wo_ps hbo_done st2 rs2 xn2_done row2_done x2_ps x2_done "
             "lg_ps lg_done").split())
        gsub, gexp, oh_done, rank_ps, slot_done, xlist_done, wd_done, wdt_ps, wdt_done, bl_ps, y0_done = (
            sem(n) for n in ("gsub gexp oh_done rank_ps slot_done xlist_done wd_done wdt_ps wdt_done "
                             "bl_ps y0_done").split())
        (x_ps, x_done, l1_ps, c1_done, ta_ps, a1_done, g1_done, l2_ps, c2_done, tb_ps, a2_done, g2_done,
         l3_ps, z_done, o_ps, o_done) = (sem(n) for n in (
             "x_ps x_done l1_ps c1_done ta_ps a1_done g1_done l2_ps c2_done tb_ps a2_done g2_done "
             "l3_ps z_done o_ps o_done").split())
        s_held, s_sums = sem("s_held"), sem("s_sums")
        s_pool = sem("s_pool")

        block = ctx.enter_context(nc.Block())

        def nothing(t):
            pass

        def in_step(step, stages):
            return [(fn, step - s) for s, fn in reversed(list(enumerate(stages))) if 0 <= step - s < TILES]

        @block.sync
        def _(sp):
            def load_lo(pair, s):
                sp.dma_start(ring[:, s, 0:LO], experts_d[pair, :, 0:LO]).then_inc(s_lo[s], 16)

            def load_hi(pair, s):
                sp.dma_start(ring[:, s, LO:WC], experts_d[pair, :, LO:WC]).then_inc(s_hi[s], 16)

            def load_rows(unit_, s):
                sp.dma_start(xs[:, s, :], by_unit[:, bass.ds(unit_, 1), :].rearrange("p u c -> p (u c)"))\
                    .then_inc(s_xs[s], 16)

            by_unit = slots_d.rearrange("(u p) c -> p u c", p=P)
            sp.dma_start(xp[:, 0, :], xp_d[0]).then_inc(s_xp[0], 16)
            sp.dma_start(wt[:], wt_d).then_inc(s_wt, 16)
            sp.dma_start(cst[:], consts_d).then_inc(s_cst, 16)
            sp.dma_start(rows[:], rows_d.partition_broadcast(P)).then_inc(s_rows, 16)
            sp.dma_start(xp[:, 1, :], xp_d[1]).then_inc(s_xp[1], 16)
            sp.dma_start(wqk0[:], wqk_d[0:D0]).then_inc(s_wqkv, 16)
            sp.dma_start(wqk1[:], wqk_d[D0:D]).then_inc(s_wqkv, 16)
            sp.dma_start(wv0[:], wv_d[0:D0]).then_inc(s_wqkv, 16)
            sp.dma_start(wv1[:], wv_d[D0:D]).then_inc(s_wqkv, 16)
            for half in range(2):
                sp.dma_start(bv[64 * half:64 * half + 64, :],
                             bv_d[half].partition_broadcast(64)).then_inc(s_wqkv, 16)
            for t in range(2, TILES):
                sp.dma_start(xp[:, t, :], xp_d[t]).then_inc(s_xp[t], 16)
            for dst, src in ((wo0[:], wo_d[0:D0]), (wo1[:], wo_d[D0:D]), (g0[:], gate_d[0:D0]),
                             (g1[:], gate_d[D0:D]), (b12[:], b12_d), (b3[:], b3_d), (bl[:], bl_d)):
                sp.dma_start(dst, src).then_inc(s_late, 16)
            for u in range(RING):
                load_lo(u, u)
                load_hi(u, u)
                if u == 1:
                    sp.wait_ge(s_set, 11)
                    sp.dma_start(slots_d.rearrange("(u p) c -> p u c", p=P),
                                 blank[:].unsqueeze(1).to_broadcast([P, UNITS + EXTRA, ROW])).then_inc(s_blank, 16)
            sp.wait_ge(s_scat, 16 * 2 * TILES)
            for u in range(RING):
                load_rows(u, u)
            sp.dma_start(sums_d[TOKENS:TOKENS + P, :], blank[:, 0:D]).then_inc(s_sums, 16)
            sp.wait_ge(y0_done, 1)
            for t in range(0, TILES, 2):
                sp.dma_start(sums_d.rearrange("(t p) d -> p t d", p=P)[:, t:t + 2, :], y0[:, t:t + 2, :])\
                    .then_inc(s_sums, 16)
            with sp.Fori(1, UNITS // RING) as g:
                for s in range(RING):
                    before = g * RING + (s - RING + 1)
                    sp.wait_ge(l1_ps, before)
                    load_lo(g * RING + s, s)
                    sp.wait_ge(o_done, before)
                    load_rows(g * RING + s, s)
                    load_hi(g * RING + s, s)
            sp.wait_ge(xlist_done, 1)
            extra = sp.value_load(xlist[0:1, EXTRA:EXTRA + 1], min_val=0, max_val=EXTRA)
            with sp.If(extra > 0):
                pair = sp.value_load(xlist[0:1, 0:1], min_val=0, max_val=UNITS - 1)
                sp.wait_ge(o_done, UNITS - RING + 1)
                load_rows(UNITS, 0)
                load_lo(pair, 0)
                load_hi(pair, 0)
            with sp.If(extra > 1):
                with sp.Fori(1, extra) as j:
                    pair = sp.value_load(xlist[0:1, bass.ds(j, 1)], min_val=0, max_val=UNITS - 1)
                    sp.wait_ge(o_done, j + UNITS)
                    load_rows(j + UNITS, 0)
                    load_lo(pair, 0)
                    load_hi(pair, 0)

        @block.gpsimd
        def _(pool):
            finished = []

            def done(ins, signal):
                ins.then_inc(signal, 1)
                finished.append(signal)
                pool.wait_ge(signal, finished.count(signal))

            done(pool.memset(vbd[:], 0.0), s_set)
            vr = vbd[:].rearrange("p t i (c v) -> p (t i c) v", v=VC)
            done(pool.memset(vr[0:64, :, HD:HD + 1], 1.0), s_set)
            done(pool.memset(vr[64:P, :, VC - 1:VC], 1.0), s_set)
            done(pool.memset(halfneg[:], -0.5), s_set)
            done(pool.memset(qT[D1:P, :, 1, :], 0.0), s_set)
            done(pool.memset(kx1[D1:P], 0.0), s_set)
            done(pool.memset(blank[:, 0:D + 1], 0.0), s_set)
            done(pool.memset(onesb[:], 1.0), s_set)
            done(pool.memset(xt[:], 0.0), s_set)
            done(pool.memset(zbd[:], 0.0), s_set)
            pool.wait_ge(s_cst, 16)
            done(pool.tensor_copy(blank[:, D + 1:ROW], const(C_TOK)[:, TILES:TILES + 1]), s_set)

            def inverse_root(t, stat, ready):
                pool.wait_ge(stat, t + 1)
                done(pool.tensor_scalar(rstd[:, t:t + 1], mv[:, t, 1:2], EPS, None, ALU.add), s_pool)
                done(pool.tensor_tensor(rstd[:, t:t + 1], rstd[:, t:t + 1], halfneg[:], ALU.pow), ready)

            def ln1(t):
                inverse_root(t, st1, rs1)

            def rope_cos(t):
                pool.wait_ge(qkb_done, t + 1)
                if t >= 2:
                    pool.wait_ge(rot_done, t - 1)
                done(pool.tensor_tensor(rcos[:, t % 2, :].rearrange("p (a n d) -> p a n d", a=2, d=HD),
                                   qkb[:, t % 2, :].rearrange("p (a n d) -> p a n d", a=2, d=HD),
                                   const(C_COS).rearrange("p (a d) -> p a d", a=2).unsqueeze(2)
                                   .to_broadcast([P, 2, HEADS, HD]), ALU.mult), cos_done)

            def hbo_add(t):
                pool.wait_ge(xn_done, t + 1)
                done(pool.tensor_tensor(h[:, t, :], h[:, t, :], rows[:, 3 * D:4 * D], ALU.add), hbo_done)

            def ln2(t):
                inverse_root(t, st2, rs2)

            pool.wait_ge(s_rows, 16)
            pool.wait_ge(s_cst, 16)
            for step in range(TILES + 8):
                for stage, t in in_step(step, [ln1, nothing, rope_cos, hbo_add, nothing, nothing, nothing,
                                               nothing, ln2]):
                    stage(t)

            pool.wait_ge(s_blank, 16)
            pool.wait_ge(row2_done, TILES)
            pool.wait_ge(slot_done, 2)
            for sl, row in ((sl1, row1), (sl2, row2)):
                for t in range(TILES):
                    pool.indirect_dma_start(slots_d, bass.IndirectOffsetOnAxis(ap=sl[:, t:t + 1], axis=0),
                                            row[:, t, :], None).then_inc(s_scat, 16)

            def sums_free(adds, holds):
                pool.wait_ge(s_held, holds)
                if not (isinstance(adds, int) and adds == 0):
                    pool.wait_ge(s_add, adds)
                pool.tensor_tensor(held[:], halfneg[0:1, :], halfneg[0:1, :], ALU.add).then_inc(s_held, 1)

            def add_rows(u, b):
                pool.wait_ge(o_done, u + 1)
                for k, ix in enumerate((ixa, ixb)):
                    sums_free(u * 32 + 16 * k, u * 2 + (k + 2))
                    pool.indirect_dma_start(sums_d, bass.IndirectOffsetOnAxis(ap=ix[:, b:b + 1], axis=0),
                                            ob[:, b, :], None, compute_op=ALU.add).then_inc(s_add, 16)

            pool.memset(held[:], 0.0).then_inc(s_held, 2)
            pool.wait_ge(s_sums, 48)
            add_rows(0, 0)
            with pool.Fori(0, UNITS // 2 - 1) as g:
                add_rows(g * 2 + 1, 1)
                add_rows(g * 2 + 2, 0)
            add_rows(UNITS - 1, 1)
            pool.wait_ge(xlist_done, 1)
            extra = pool.value_load(xlist[0:1, EXTRA:EXTRA + 1], min_val=0, max_val=EXTRA)
            with pool.If(extra > 0):
                with pool.Fori(0, extra) as j:
                    add_rows(j + UNITS, 0)
            sums_free(extra * 32 + UNITS * 32, extra * 2 + (UNITS * 2 + 2))
            pool.dma_start(out_d, sums_d[0:TOKENS, :]).then_inc(s_out, 16)
            pool.wait_ge(s_out, 16)

        @block.scalar
        def _(act):
            act.wait_ge(s_cst, 16)
            act.activation(identb[:], ident, ACT.Copy)
            act.activation(trib[:], const(C_TRI), ACT.Copy)
            act.activation(causb[:], const(C_CAUS).unsqueeze(1).to_broadcast([P, H0, SEQ]),
                           ACT.Copy).then_inc(s_cast, 1)
            act.wait_ge(s_set, 11)

            def copies(dst, src_bank, t, ready, done):
                act.wait_ge(ready, t + 1)
                act.activation(dst[:, t % 2, 0, :], src_bank[:, 0:P], ACT.Copy)
                act.activation(dst[0:D1, t % 2, 1, :], src_bank[0:D1, P:2 * P], ACT.Copy).then_inc(done, 1)

            def xn_t(t):
                if t >= 2:
                    act.wait_ge(v_ps, t - 1)
                copies(xnT, bank[2], t, xnt_ps, xnt_done)

            def q_t(t):
                if t >= 2:
                    act.wait_ge(sc_ps, t - 1)
                copies(qT, bank[6], t, qt_ps, qt_done)
                for n in range(H1):
                    last = act.activation(
                        kx1[0:D1, t % 2].rearrange("p i (n s) -> p i n s", s=SEQ)[:, :, n, :],
                        bank[6][0:D1, 2 * P:3 * P].rearrange("p (i s) -> p i s", s=SEQ),
                        ACT.Copy, scale=const(C_M1)[0:D1, n:n + 1])
                last.then_inc(kx1_done, 1)

            def exp_s(t):
                if t >= 2:
                    act.wait_ge(pt_ps, t - 1)
                act.wait_ge(sub_done, t + 1)
                act.activation(prob[:, t % 2, :], ssub[:], ACT.Exp).then_inc(exp_done, 1)

            def p_t(t):
                if t >= 2:
                    act.wait_ge(pv_ps, t - 1)
                act.wait_ge(pt_ps, t + 1)
                act.activation(pT[:, t % 2, 0:4 * P], bank[2][:], ACT.Copy)
                act.activation(pT[:, t % 2, 4 * P:6 * P], bank[3][:, 0:2 * P], ACT.Copy).then_inc(pt_done, 1)

            def att_t(t):
                if t >= 2:
                    act.wait_ge(wo_ps, t - 1)
                copies(attT, bank[6], t, at_ps, at_done)

            def rows2(t):
                act.wait_ge(xn2_done, t + 1)
                act.activation(row2[:, t, 0:D], row1[:, t, 0:D], ACT.Copy).then_inc(row2_done, 1)

            def xn2_t(t):
                if t >= 2:
                    act.wait_ge(lg_ps, t - 1)
                copies(xn2T, bank[2], t, x2_ps, x2_done)
                rows2(t)

            for step in range(TILES + 10):
                for stage, t in in_step(step, [nothing, xn_t, nothing, q_t, exp_s, p_t, nothing, att_t,
                                               nothing, xn2_t, nothing]):
                    stage(t)

            act.wait_ge(gsub, 1)
            act.activation(ge[:], gs[:], ACT.Exp).then_inc(gexp, 1)

            def copy_1(u):
                act.wait_ge(l1_ps, u + 1)
                act.activation(pre1[:], bank[1][:], ACT.Copy).then_inc(c1_done, 1)

            def copy_2(u):
                act.wait_ge(l2_ps, u + 1)
                act.activation(pre2[:], bank[2][:], ACT.Copy).then_inc(c2_done, 1)

            def gelu_1(u):
                act.wait_ge(a1_done, u + 1)
                act.activation(h1T_, hb1[:], ACT.Gelu).then_inc(g1_done, 1)

            def gelu_2(u):
                act.wait_ge(a2_done, u + 1)
                act.activation(h2T_, hb2[:], ACT.Gelu).then_inc(g2_done, 1)

            def unit(u, more):
                copy_2(u)
                if more:
                    copy_1(u + 1)
                gelu_2(u)
                if more:
                    gelu_1(u + 1)

            copy_1(0)
            gelu_1(0)
            with act.Fori(0, UNITS - 1) as u:
                unit(u, True)
            unit(UNITS - 1, False)
            act.wait_ge(xlist_done, 1)
            extra = act.value_load(xlist[0:1, EXTRA:EXTRA + 1], min_val=0, max_val=EXTRA)
            with act.If(extra > 0):
                with act.Fori(0, extra) as j:
                    copy_1(j + UNITS)
                    gelu_1(j + UNITS)
                    copy_2(j + UNITS)
                    gelu_2(j + UNITS)

        @block.vector
        def _(dve):
            chain = [0]

            def link(ins):
                chain[0] += 1
                ins.then_inc(s_v, 1)
                dve.wait_ge(s_v, chain[0])

            def ln1_a(t):
                dve.wait_ge(embedded, t + 1)
                ins = dve.tensor_tensor(h[:, t, :], bank[t % 2][:, 0:D], rows[:, 0:D], ALU.add)
                ins.then_inc(h_done, 1)
                dve.wait_ge(h_done, t + 1)
                link(dve.bn_stats(stats[:, t, :], h[:, t, :]))
                dve.bn_aggr(mv[:, t, :], stats[:, t, :]).then_inc(st1, 1)

            def ln1_b(t):
                dve.wait_ge(rs1, t + 1)
                if t >= 2:
                    dve.wait_ge(xnt_ps, t - 1)
                dve.wait_ge(st1, t + 1)
                dve.tensor_scalar(xn[:, t % 2, :], h[:, t, :], mv[:, t, 0:1], rstd[:, t:t + 1],
                                  ALU.subtract, ALU.mult).then_inc(xn_done, 1)

            def qkv(t):
                dve.wait_ge(qk_ps, t + 1)
                if t >= 2:
                    dve.wait_ge(cos_done, t - 1)
                dve.tensor_tensor(qkb[:, t % 2, :], bank[4][:, 0:2 * D], rows[:, D:3 * D], ALU.add)\
                    .then_inc(qkb_done, 1)
                dve.wait_ge(v_ps, t + 1)
                for half in range(2):
                    q = slice(64 * half, 64 * half + 64)
                    c = (HD + 1) * half
                    last = dve.tensor_tensor(
                        vbd[q, t].rearrange("p i (c v) -> p i c v", v=VC)[:, :, :, c:c + HD],
                        bank[5][q, 0:2 * HP * HD].rearrange("p (i c d) -> p i c d", i=2, d=HD),
                        bv[q, :].rearrange("p (c d) -> p c d", d=HD).unsqueeze(1)
                        .to_broadcast([64, 2, HP, HD]), ALU.add)
                last.then_inc(v_done, 1)
                dve.wait_ge(qkb_done, t + 1)
                half_ = HD // 2
                src = qkb[:, t % 2, :].rearrange("p (a n d) -> p a n d", a=2, d=HD)
                dst = rsin[:].rearrange("p (a n d) -> p a n d", a=2, d=HD)
                sin = const(C_SIN).rearrange("p (a d) -> p a d", a=2).unsqueeze(2)\
                    .to_broadcast([P, 2, HEADS, HD])
                if t >= 1:
                    dve.wait_ge(rot_done, t)
                dve.tensor_tensor(dst[:, :, :, 0:half_], src[:, :, :, half_:HD], sin[:, :, :, 0:half_], ALU.mult)
                link(dve.tensor_tensor(dst[:, :, :, half_:HD], src[:, :, :, 0:half_], sin[:, :, :, half_:HD],
                                       ALU.mult))
                dve.wait_ge(cos_done, t + 1)
                if t >= 2:
                    dve.wait_ge(kt_ps, t - 1)
                dve.tensor_tensor(rot[:, t % 2, :], rcos[:, t % 2, :], rsin[:], ALU.add).then_inc(rot_done, 1)

            def keys(t):
                dve.wait_ge(kt_ps, t + 1)
                if t >= 2:
                    dve.wait_ge(sc_ps, t - 1)
                for i in range(2):
                    last = dve.tensor_tensor(
                        kx0[:, t % 2, i, :].rearrange("p (n s) -> p n s", s=SEQ),
                        bank[7][:, i * SEQ:(i + 1) * SEQ].unsqueeze(1).to_broadcast([P, H0, SEQ]),
                        const(C_M0).unsqueeze(2).to_broadcast([P, H0, SEQ]), ALU.mult)
                last.then_inc(kx0_done, 1)

            def scores(t):
                dve.wait_ge(sc_ps, t + 1)
                m = smax[:, t % 2, :]
                s0 = bank[0][:].rearrange("p (n s) -> p n s", s=SEQ)
                s1 = bank[1][:, 0:H1 * SEQ].rearrange("p (n s) -> p n s", s=SEQ)
                dve.tensor_reduce(m[:, 0:H0], s0, AX.X, ALU.max)
                link(dve.tensor_reduce(m[:, H0:HEADS], s1, AX.X, ALU.max))
                if t >= 1:
                    dve.wait_ge(exp_done, t)
                out = ssub[:].rearrange("p (n s) -> p n s", s=SEQ)
                dve.tensor_tensor(out[:, 0:H0, :], s0, m[:, 0:H0].unsqueeze(2).to_broadcast([P, H0, SEQ]), ALU.subtract)
                dve.tensor_tensor(out[:, H0:HEADS, :], s1, m[:, H0:HEADS].unsqueeze(2).to_broadcast([P, H1, SEQ]),
                                  ALU.subtract).then_inc(sub_done, 1)

            def attend(t):
                dve.wait_ge(pv_ps, t + 1)
                pv = bank[4][:, 0:HP * VC].rearrange("p (n v) -> p n v", v=HD + 1)
                if t >= 2:
                    dve.wait_ge(at_ps, t - 1)
                link(dve.reciprocal(rden[:, t % 2, :], pv[:, :, HD]))
                dve.tensor_tensor(att[:, t % 2, :].rearrange("p (n d) -> p n d", d=HD), pv[:, :, 0:HD],
                                  rden[:, t % 2, :].unsqueeze(2).to_broadcast([P, HEADS, HD]), ALU.mult)\
                    .then_inc(att_done, 1)

            def ln2_a(t):
                dve.wait_ge(wo_ps, t + 1)
                dve.wait_ge(hbo_done, t + 1)
                link(dve.tensor_tensor(h2[:, t, :], bank[0][:, 0:D], h[:, t, :], ALU.add))
                link(dve.bn_stats(stats[:, t, :], h2[:, t, :]))
                dve.bn_aggr(mv[:, t, :], stats[:, t, :]).then_inc(st2, 1)

            def ln2_b(t):
                dve.wait_ge(rs2, t + 1)
                dve.wait_ge(st2, t + 1)
                dve.tensor_scalar(row1[:, t, 0:D], h2[:, t, :], mv[:, t, 0:1], rstd[:, t:t + 1],
                                  ALU.subtract, ALU.mult).then_inc(xn2_done, 1)

            def logits(t):
                dve.wait_ge(lg_ps, t + 1)
                dve.tensor_copy(lg[:, t, :], bank[4][:, 0:E]).then_inc(lg_done, 1)

            def first(t):
                ln1_a(t)
                ln1_b(t)

            def second(t):
                ln2_a(t)
                ln2_b(t)

            dve.wait_ge(s_rows, 16)
            dve.wait_ge(s_cst, 16)
            dve.wait_ge(s_set, 11)
            dve.wait_ge(s_wqkv, 96)
            for step in range(TILES + 10):
                for stage, t in in_step(step, [first, nothing, qkv, keys, scores, nothing, attend, nothing,
                                               second, nothing, logits]):
                    stage(t)

            dve.wait_ge(lg_done, TILES)
            m, z, rz, den, w1, w2, sf = (s4[:, i, :] for i in range(7))
            wide = [P, TILES, E]
            link(dve.tensor_reduce(m, lg[:], AX.X, ALU.max))
            dve.tensor_tensor(gs[:], lg[:], m.unsqueeze(2).to_broadcast(wide), ALU.subtract).then_inc(gsub, 1)
            dve.wait_ge(gexp, 1)
            link(dve.tensor_reduce(z, ge[:], AX.X, ALU.add))
            link(dve.reciprocal(rz, z))
            link(dve.tensor_tensor(prb[:], ge[:], rz.unsqueeze(2).to_broadcast(wide), ALU.mult))
            for t in range(TILES):
                last = dve.max(top[:, t, :], prb[:, t, :])
            link(last)
            for t in range(TILES):
                last = dve.max_index(topi[:, t, :], top[:, t, :], prb[:, t, :])
            link(last)
            link(dve.tensor_copy(topf[:], topi[:, :, 0:2]))
            iota = const(C_IOTA)
            for k, oh in enumerate((oh1, oh2)):
                last = dve.tensor_tensor(oh[:], iota.unsqueeze(1).to_broadcast(wide),
                                         topf[:, :, k:k + 1].to_broadcast(wide), ALU.is_equal)
            link(last)
            dve.tensor_tensor(ohb[:], oh1[:], oh2[:], ALU.add).then_inc(oh_done, 1)
            link(dve.tensor_tensor(den, top[:, :, 0], top[:, :, 1], ALU.add))
            link(dve.tensor_scalar(den, den, 1e-20, None, ALU.add))
            link(dve.reciprocal(rz, den))
            dve.tensor_tensor(w1, top[:, :, 0], rz, ALU.mult)
            link(dve.tensor_tensor(w2, top[:, :, 1], rz, ALU.mult))
            tok = const(C_TOK)[:, 0:TILES]
            for row, w in ((row1, w1), (row2, w2)):
                dve.tensor_copy(row[:, :, D], w)
                last = dve.tensor_copy(row[:, :, D + 1], tok)
            link(last)
            dve.wait_ge(rank_ps, 2)
            link(dve.tensor_scalar(cnti[:], bank[5][:, 0:E], float(CAP - 1), None, ALU.add))
            link(dve.tensor_scalar(cnti[:], cnti[:], 6, None, ALU.logical_shift_right))
            pairs = cnti[:].rearrange("p (u e) -> p u e", e=2)
            a, b, base, incl = (xtra[:, i, :] for i in range(4))
            link(dve.tensor_tensor(a, pairs[:, :, 0], pairs[:, :, 1], ALU.max))
            link(dve.tensor_scalar(a, a, 1.0, -1.0, ALU.max, ALU.add))
            src, dst, shift = a, b, 1
            while shift < UNITS:
                dve.tensor_copy(dst[:, 0:shift], src[:, 0:shift])
                link(dve.tensor_tensor(dst[:, shift:UNITS], src[:, shift:UNITS], src[:, 0:UNITS - shift], ALU.add))
                src, dst, shift = dst, (incl if dst is b else b), shift * 2
            incl_ = src
            base = xtra[:, 4, :]
            dve.memset(base[:, 0:1], 0.0)
            link(dve.tensor_copy(base[:, 1:UNITS], incl_[:, 0:UNITS - 1]))
            link(dve.tensor_tensor(base, base, const(C_PAIR), ALU.subtract))
            for e in range(2):
                last = dve.tensor_scalar(bext[:].rearrange("p (u e) -> p u e", e=2)[:, :, e], base,
                                         float(UNITS - 1), float(P), ALU.add, ALU.mult)
            link(last)
            rank = bank[7][:, 0:TILES * E]
            tmp = [rtmp[:, i, :].rearrange("p (t e) -> p t e", e=E) for i in range(6)]
            rk = rank.rearrange("p (t e) -> p t e", e=E)
            dve.tensor_copy(ranki[:], rk)
            link(dve.tensor_scalar(tmp[0], rk, float(CAP), None, ALU.is_ge))
            dve.tensor_scalar(ranki[:], ranki[:], 6, 6, ALU.logical_shift_right, ALU.logical_shift_left)
            link(dve.tensor_tensor(tmp[1], tmp[0], bext[:].unsqueeze(1).to_broadcast(wide), ALU.mult))
            link(dve.tensor_tensor(tmp[2], rk, tmp[1], ALU.add))
            link(dve.tensor_tensor(tmp[3], tmp[2], ranki[:], ALU.add))
            link(dve.scalar_tensor_tensor(tmp[4], iota.unsqueeze(1).to_broadcast(wide), float(CAP), tmp[3],
                                          ALU.mult, ALU.add))
            for k, (oh, sl) in enumerate(((oh1, sl1), (oh2, sl2))):
                link(dve.tensor_tensor(tmp[5], tmp[4], oh[:], ALU.mult))
                link(dve.tensor_reduce(sf, tmp[5], AX.X, ALU.add))
                dve.tensor_copy(sl[:], sf).then_inc(slot_done, 1)
                dve.wait_ge(slot_done, k + 1)
            link(dve.tensor_tensor(xtab, incl_[0:1, :].unsqueeze(1).to_broadcast([1, EXTRA, UNITS]),
                                   iota[0:1, 0:EXTRA].unsqueeze(2).to_broadcast([1, EXTRA, UNITS]), ALU.is_le))
            link(dve.tensor_reduce(xcount[:], xtab, AX.X, ALU.add))
            link(dve.tensor_scalar(xcount[:], xcount[:], float(UNITS - 1), None, ALU.min))
            dve.tensor_copy(xlist[:, 0:EXTRA], xcount[:])
            dve.tensor_copy(xlist[:, EXTRA:EXTRA + 1], incl_[0:1, UNITS - 1:UNITS]).then_inc(xlist_done, 1)
            dve.tensor_tensor(tmp[0], oh1[:], w1.unsqueeze(2).to_broadcast(wide), ALU.mult)
            link(dve.tensor_tensor(tmp[1], oh2[:], w2.unsqueeze(2).to_broadcast(wide), ALU.mult))
            dve.tensor_tensor(wd[:], tmp[0], tmp[1], ALU.add).then_inc(wd_done, 1)
            dve.wait_ge(wdt_ps, 1)
            dve.tensor_copy(prob[0:E, 1, 0:TILES * P], bank[6][0:E, :]).then_inc(wdt_done, 1)
            dve.wait_ge(bl_ps, 1)
            for t in range(TILES):
                last = dve.tensor_tensor(y0[:, t, :], bank[t // 2 + 2][:, (t % 2) * D:(t % 2 + 1) * D],
                                         h2[:, t, :], ALU.add)
            last.then_inc(y0_done, 1)

            def rows_in(u, b):
                dve.wait_ge(x_ps, u + 1)
                dve.tensor_copy(xm[:, b, :], bank[0][:, 64:64 + P])
                dve.tensor_copy(xt[0:64, b, 0:64], bank[0][0:64, 0:64])
                dve.tensor_copy(xt[64:P, b, 64:P], bank[0][64:P, P + 64:2 * P]).then_inc(x_done, 1)

            def add_bias(u, pair, k, out, bank_, ready, done):
                dve.wait_ge(ready, u + 1)
                dve.tensor_tensor(out[:].rearrange("p (k s) -> p k s", s=CAP),
                                  bank_[:].rearrange("p (k s) -> p k s", s=CAP),
                                  pair_bias(pair, k).to_broadcast([P, 2 * HT, CAP]), ALU.add).then_inc(done, 1)

            def pair_bias(pair, k):
                return b12[:, bass.ds(pair, 1), k, :].rearrange("p u k -> p (u k)").unsqueeze(2)

            def bottle(u, pair):
                dve.wait_ge(l3_ps, u + 1)
                for half in range(2):
                    q = slice(64 * half, 64 * half + 64)
                    last = dve.tensor_scalar(zbd[q, q], bank[5][q, 0:CAP], b3[q, bass.ds(pair, 1)], None, ALU.add)
                last.then_inc(z_done, 1)

            def results(u, s, b):
                dve.wait_ge(o_ps, u + 1)
                dve.wait_ge(s_held, u * 2 + 1)
                dve.tensor_scalar(ixa[:, b:b + 1], xs[:, s, D + 1:ROW], const(C_OFFA), None, ALU.max)
                dve.tensor_scalar(ixb[:, b:b + 1], xs[:, s, D + 1:ROW], const(C_OFFB), None, ALU.max)
                dve.tensor_scalar(ob[:, b, :], bank[6][:, 0:D], xs[:, s, D:D + 1], None, ALU.mult)\
                    .then_inc(o_done, 1)

            def unit(u, s, more, more2):
                add_bias(u, u, 1, hb2, bank[4], tb_ps, a2_done)
                if more:
                    add_bias(u + 1, u + 1, 0, hb1, bank[3], ta_ps, a1_done)
                bottle(u, u)
                if more2:
                    rows_in(u + 2, s % 2)
                results(u, s, s % 2)

            dve.wait_ge(s_late, 16 * 7)
            rows_in(0, 0)
            rows_in(1, 1)
            add_bias(0, 0, 0, hb1, bank[3], ta_ps, a1_done)
            with dve.Fori(0, UNITS // RING - 1) as g:
                for s in range(RING):
                    unit(g * RING + s, s, True, True)
            for s in range(RING):
                unit(UNITS - RING + s, s, s + 1 < RING, s + 2 < RING)
            dve.wait_ge(xlist_done, 1)
            extra = dve.value_load(xlist[0:1, EXTRA:EXTRA + 1], min_val=0, max_val=EXTRA)
            with dve.If(extra > 0):
                with dve.Fori(0, extra) as j:
                    pair = dve.value_load(xlist[0:1, bass.ds(j, 1)], min_val=0, max_val=UNITS - 1)
                    u = j + UNITS
                    rows_in(u, 0)
                    add_bias(u, pair, 0, hb1, bank[3], ta_ps, a1_done)
                    add_bias(u, pair, 1, hb2, bank[4], tb_ps, a2_done)
                    bottle(u, pair)
                    dve.wait_ge(s_add, u * 32)
                    results(u, 0, 0)

        @block.tensor
        def _(pe):
            mm, tr = nc.tensor.matmul, nc.tensor.transpose

            def channels_t(src, out_bank):
                tr(out_bank[:, 0:P], src[:, 0:D0], ident)
                return tr(out_bank[0:D1, P:2 * P], src[:, D0:D], ident)

            def embed(t):
                pe.wait_ge(s_xp[t], 16)
                if t >= 2:
                    pe.wait_ge(h_done, t - 1)
                for k in range(KT):
                    last = mm(bank[t % 2][:, 0:D], xp[:, t, k * P:(k + 1) * P], wt[:, k, :],
                              start=k == 0, stop=k == KT - 1)
                last.then_inc(embedded, 1)

            def xn_t(t):
                pe.wait_ge(xn_done, t + 1)
                if t >= 1:
                    pe.wait_ge(xnt_done, t)
                channels_t(xn[:, t % 2, :], bank[2]).then_inc(xnt_ps, 1)

            def qkv(t):
                if t >= 1:
                    pe.wait_ge(qkb_done, t)
                    pe.wait_ge(v_done, t)
                pe.wait_ge(xnt_done, t + 1)
                mm(bank[4][:, 0:2 * D], xnT[:, t % 2, 0, :], wqk0[:], start=True, stop=False)
                mm(bank[4][:, 0:2 * D], xnT[0:D1, t % 2, 1, :], wqk1[:], start=False, stop=True)\
                    .then_inc(qk_ps, 1)
                for i in range(2):
                    for half in range(2):
                        o = bank[5][64 * half:64 * half + 64, i * 96:(i + 1) * 96]
                        c = slice(96 * half, 96 * half + 96)
                        mm(o, xnT[:, t % 2, 0, i * 64:(i + 1) * 64], wv0[:, c], start=True, stop=False)
                        last = mm(o, xnT[0:D1, t % 2, 1, i * 64:(i + 1) * 64], wv1[:, c], start=False, stop=True)
                last.then_inc(v_ps, 1)

            def qk_t(t):
                pe.wait_ge(rot_done, t + 1)
                if t >= 1:
                    pe.wait_ge(kx1_done, t)
                    pe.wait_ge(kx0_done, t)
                r = rot[:, t % 2, :]
                channels_t(r[:, 0:D], bank[6])
                tr(bank[6][0:D1, 2 * P:3 * P], r[:, D + D0:2 * D], ident).then_inc(qt_ps, 1)
                tr(bank[7][:, 0:P], r[:, D:D + D0], ident).then_inc(kt_ps, 1)

            def scores(t):
                if t == 0:
                    pe.wait_ge(h_done, TILES)
                    pe.wait_ge(s_cast, 1)
                else:
                    pe.wait_ge(sub_done, t)
                causal = causb[:].rearrange("p n s -> p (n s)")
                mm(bank[0][:], identb[:], causal, start=True, stop=False, skip_group_check=True)
                mm(bank[1][:, 0:H1 * SEQ], identb[:], causal[:, 0:H1 * SEQ], start=True, stop=False,
                   skip_group_check=True)
                pe.wait_ge(kx1_done, t + 1)
                pe.wait_ge(kx0_done, t + 1)
                for i in range(2):
                    q = slice(64 * i, 64 * i + 64)
                    mm(bank[0][q, :], qT[:, t % 2, 0, q], kx0[:, t % 2, i, :], start=False, stop=True,
                       skip_group_check=True)
                for i in range(2):
                    q = slice(64 * i, 64 * i + 64)
                    last = mm(bank[1][q, 0:H1 * SEQ], qT[:, t % 2, 1, q], kx1[:, t % 2, i, :], start=False,
                              stop=True, skip_group_check=True)
                last.then_inc(sc_ps, 1)

            def p_t(t):
                pe.wait_ge(xnt_done, TILES) if t == 0 else pe.wait_ge(pt_done, t)
                pe.wait_ge(exp_done, t + 1)
                for c in range(HP):
                    last = tr(bank[2 + c // 4][:, (c % 4) * P:(c % 4 + 1) * P],
                              prob[:, t % 2, c * P:(c + 1) * P], ident)
                last.then_inc(pt_ps, 1)

            def values(t):
                if t == 0:
                    pe.wait_ge(qkb_done, TILES)
                else:
                    pe.wait_ge(att_done, t)
                pe.wait_ge(v_done, t + 1)
                pe.wait_ge(pt_done, t + 1)
                for c in range(HP):
                    for i in range(2):
                        q = slice(64 * i, 64 * i + 64)
                        last = mm(bank[4][q, c * VC:(c + 1) * VC],
                                  pT[:, t % 2, c * P + 64 * i:c * P + 64 * i + 64],
                                  vbd[:, t, i, c * VC:(c + 1) * VC], start=True, stop=True)
                last.then_inc(pv_ps, 1)

            def att_t(t):
                pe.wait_ge(kx1_done, TILES) if t == 0 else pe.wait_ge(at_done, t)
                pe.wait_ge(att_done, t + 1)
                channels_t(att[:, t % 2, :], bank[6]).then_inc(at_ps, 1)

            def project(t):
                if t == 0:
                    pe.wait_ge(sub_done, TILES)
                    pe.wait_ge(s_late, 16 * 7)
                else:
                    pe.wait_ge(st2, t)
                pe.wait_ge(at_done, t + 1)
                mm(bank[0][:, 0:D], attT[:, t % 2, 0, :], wo0[:], start=True, stop=False)
                mm(bank[0][:, 0:D], attT[0:D1, t % 2, 1, :], wo1[:], start=False, stop=True).then_inc(wo_ps, 1)

            def xn2_t(t):
                pe.wait_ge(pt_done, TILES) if t == 0 else pe.wait_ge(x2_done, t)
                pe.wait_ge(xn2_done, t + 1)
                channels_t(row1[:, t, 0:D], bank[2]).then_inc(x2_ps, 1)

            def gate(t):
                pe.wait_ge(att_done, TILES) if t == 0 else pe.wait_ge(lg_done, t)
                pe.wait_ge(x2_done, t + 1)
                mm(bank[4][:, 0:E], xn2T[:, t % 2, 0, :], g0[:], start=True, stop=False)
                mm(bank[4][:, 0:E], xn2T[0:D1, t % 2, 1, :], g1[:], start=False, stop=True).then_inc(lg_ps, 1)

            pe.wait_ge(s_wt, 16)
            pe.wait_ge(s_cst, 16)
            pe.wait_ge(s_wqkv, 96)
            for step in range(TILES + 10):
                for stage, t in in_step(step, [embed, xn_t, qkv, qk_t, scores, p_t, values, att_t, project,
                                               xn2_t, gate]):
                    stage(t)

            pe.wait_ge(oh_done, 1)
            for t in range(TILES):
                o = bank[7][:, t * E:(t + 1) * E]
                for t2 in range(t + 1):
                    last = mm(o, trib[:] if t2 == t else onesb[:], ohb[:, t2, :], start=t2 == 0, stop=t2 == t)
            last.then_inc(rank_ps, 1)
            for t in range(TILES):
                last = mm(bank[5][:, 0:E], onesb[:], ohb[:, t, :], start=t == 0, stop=t == TILES - 1)
            last.then_inc(rank_ps, 1)
            pe.wait_ge(wd_done, 1)
            pe.wait_ge(at_done, TILES)
            for t in range(TILES):
                last = tr(bank[6][0:E, t * P:(t + 1) * P], wd[:, t, :], ident)
            last.then_inc(wdt_ps, 1)
            pe.wait_ge(wdt_done, 1)
            for t in range(TILES):
                last = mm(bank[t // 2 + 2][:, (t % 2) * D:(t % 2 + 1) * D], wdT[:, t, :], bl[:],
                          start=True, stop=True)
            last.then_inc(bl_ps, 1)

            def rows_t(u, s, arrived):
                pe.wait_ge(s_xs[s], arrived)
                pe.wait_ge(x_done, u)
                tr(bank[0][:, 0:P], xs[:, s, 0:D0], ident)
                tr(bank[0][:, P:2 * P], xs[:, s, D1:D], ident).then_inc(x_ps, 1)

            def w1(s, c):
                return ring[:, s, c * HID:(c + 1) * HID]

            def layer_1(u, s, b, arrived):
                pe.wait_ge(x_done, u + 1)
                pe.wait_ge(s_lo[s], arrived)
                mm(bank[1][0:64, :], xm[:, b, 64:P], w1(s, 0), start=True, stop=False, skip_group_check=True)
                mm(bank[1][64:P, :], xm[:, b, 0:64], w1(s, 1), start=True, stop=False, skip_group_check=True)
                mm(bank[1][:], xt[:, b, :], w1(s, 2), start=False, stop=True, skip_group_check=True)\
                    .then_inc(l1_ps, 1)

            def hidden_t(u, pre, out_bank, ready, done):
                pe.wait_ge(ready, u + 1)
                for k in range(HT):
                    last = tr(out_bank[:, k * P:(k + 1) * P], pre[:, k * P:(k + 1) * P], ident)
                last.then_inc(done, 1)

            def layer_2(u, s, arrived):
                pe.wait_ge(s_hi[s], arrived)
                pe.wait_ge(g1_done, u + 1)
                for k in range(HT):
                    for half in range(2):
                        q = slice(64 * half, 64 * half + 64)
                        c = LO + (half * HT + k) * HID
                        last = mm(bank[2][q, :], h1T[:, k, q], ring[:, s, c:c + HID], start=k == 0,
                                  stop=k == HT - 1)
                last.then_inc(l2_ps, 1)

            def layer_3(u, s):
                pe.wait_ge(g2_done, u + 1)
                for half in range(2):
                    q = slice(64 * half, 64 * half + 64)
                    for k in range(HT):
                        c = LO + W2C + (half * HT + k) * BOT
                        last = mm(bank[5][q, 0:CAP], ring[:, s, c:c + BOT], h2T[:, k, q], start=k == 0,
                                  stop=k == HT - 1)
                last.then_inc(l3_ps, 1)

            def layer_4(u, s):
                pe.wait_ge(z_done, u + 1)
                mm(bank[6][:, 0:D], zbd[:], ring[:, s, WC - D:WC], start=True, stop=True).then_inc(o_ps, 1)

            def unit(g, s, more, more2):
                u = g * RING + s

                def arrival(ahead):
                    return (g + (s + ahead) // RING) * 16 + 16

                layer_2(u, s, arrival(0))
                if more:
                    nxt = (s + 1) % RING
                    layer_1(u + 1, nxt, nxt % 2, arrival(1))
                hidden_t(u, pre2, bank[4], c2_done, tb_ps)
                if more:
                    hidden_t(u + 1, pre1, bank[3], c1_done, ta_ps)
                layer_3(u, s)
                if more2:
                    rows_t(u + 2, (s + 2) % RING, arrival(2))
                layer_4(u, s)

            pe.wait_ge(y0_done, 1)
            rows_t(0, 0, 16)
            rows_t(1, 1, 16)
            layer_1(0, 0, 0, 16)
            hidden_t(0, pre1, bank[3], c1_done, ta_ps)
            with pe.Fori(0, UNITS // RING - 1) as g:
                for s in range(RING):
                    unit(g, s, True, True)
            for s in range(RING):
                unit(UNITS // RING - 1, s, s + 1 < RING, s + 2 < RING)
            pe.wait_ge(xlist_done, 1)
            extra = pe.value_load(xlist[0:1, EXTRA:EXTRA + 1], min_val=0, max_val=EXTRA)
            with pe.If(extra > 0):
                with pe.Fori(0, extra) as j:
                    u = j + UNITS
                    arrived = j * 16 + (UNITS // RING + 1) * 16
                    rows_t(u, 0, arrived)
                    layer_1(u, 0, 0, arrived)
                    hidden_t(u, pre1, bank[3], c1_done, ta_ps)
                    layer_2(u, 0, arrived)
                    hidden_t(u, pre2, bank[4], c2_done, tb_ps)
                    layer_3(u, 0)
                    layer_4(u, 0)


def kernel(**inputs):
    import numpy as np
    import concourse.bacc as bacc
    from concourse.bass_utils import run_bass_kernel_spmd

    a = {k: np.asarray(v) for k, v in inputs.items()}
    x = a["x"].reshape(TILES, 2, 3, 8, 16, 8, 16).transpose(0, 4, 6, 2, 1, 3, 5)
    x = x.reshape(TILES, KT, P, P).transpose(0, 2, 1, 3).reshape(TILES, P, KT * P)
    wt = a["L0_tok_W"].T.reshape(KT, P, D).transpose(1, 0, 2)
    wqk = np.concatenate([a["L0_attn_Wq"].T, a["L0_attn_Wk"].T], 1)
    wv = a["L0_attn_Wv"].T.reshape(D, HP, 2, HD).transpose(0, 2, 1, 3).reshape(D, D)
    bv = a["L0_attn_bv"].reshape(HP, 2, HD).transpose(1, 0, 2).reshape(2, HP * HD)
    rows = np.concatenate([a["L0_tok_b"], a["L0_attn_bq"], a["L0_attn_bk"], a["L0_attn_bo"]])
    w1 = a["L0_ffn_W1"].reshape(UNITS, 2, D, HID)
    tails = np.concatenate([w1[:, 0, 0:D1], w1[:, 1, D0:D]], 1)
    w2 = a["L0_ffn_W2"].reshape(UNITS, 2, HT, P, HID).transpose(0, 3, 1, 2, 4).reshape(UNITS, P, W2C)
    w3 = a["L0_ffn_W3"].reshape(UNITS, 2, HT, P, BOT).transpose(0, 3, 1, 2, 4).reshape(UNITS, P, W3C)
    wl = a["L0_ffn_Wl"].reshape(UNITS, 2 * BOT, D)
    experts = np.concatenate([w1[:, 0, D1:D], w1[:, 1, 0:D0], tails, w2, w3, wl], 2)

    def by_hidden(b):
        return b.reshape(UNITS, 2, HT, P).transpose(3, 0, 2, 1).reshape(P, UNITS, HT * 2)
    b12 = np.stack([by_hidden(a["L0_ffn_b1"]), by_hidden(a["L0_ffn_b2"])], 2)
    b3 = a["L0_ffn_b3"].reshape(UNITS, 2 * BOT).T

    c = np.zeros((P, NC_), np.float32)

    def put(i, v):
        c[:, C_AT[i]:C_AT[i + 1]] = v
    p = np.arange(P)
    put(C_ID, p[:, None] == p[None, :])
    put(C_TRI, p[:, None] < p[None, :])
    put(C_CAUS, np.where(np.arange(SEQ)[None, :] > (p % SEQ)[:, None], -1e30, 0.0))
    inv = (1.0 / 10000.0 ** (np.arange(0, HD, 2, dtype=np.float32) / np.float32(HD))).astype(np.float32)
    ang = (p % SEQ).astype(np.float32)[:, None] * inv[None, :]
    cos, sin = np.cos(ang), np.sin(ang)
    scale = 1.0 / np.sqrt(np.float32(HD))
    cos2, sin2 = np.concatenate([cos, cos], 1), np.concatenate([-sin, sin], 1)
    put(C_COS, np.concatenate([cos2 * scale, cos2], 1))
    put(C_SIN, np.concatenate([sin2 * scale, sin2], 1))
    put(C_M0, (p // HD)[:, None] == np.arange(H0)[None, :])
    put(C_M1, (p // HD)[:, None] == np.arange(H1)[None, :])
    put(C_IOTA, np.arange(E)[None, :])
    put(C_OFFA, np.where(p < 64, 0.0, TOKENS + p)[:, None])
    put(C_OFFB, np.where(p < 64, TOKENS + p, 0.0)[:, None])
    put(C_TOK, p[:, None] + P * np.arange(TILES + 1)[None, :])
    put(C_PAIR, np.arange(UNITS)[None, :])

    arrays = {"xp": x, "wt": wt, "wqk": wqk, "wv": wv, "wo": a["L0_attn_Wo"].T, "gate": a["L0_ffn_gate_w"].T,
              "rows": rows, "bv": bv, "consts": c, "experts": experts, "b12": b12, "b3": b3,
              "bl": a["L0_ffn_bl"]}
    arrays = {f"in_{k}": np.ascontiguousarray(v) for k, v in arrays.items()}
    nc = bacc.Bacc("TRN2", target_bir_lowering=False, num_devices=1)
    args = [nc.dram_tensor(k, v.shape, F32, kind="ExternalInput").ap() for k, v in arrays.items()]
    out = nc.dram_tensor("out", (TOKENS, D), F32, kind="ExternalOutput").ap()
    vit_layer(nc, *args, out)
    r = run_bass_kernel_spmd(nc, [arrays], core_ids=[0])
    return r.results[0]["out"].reshape(TILES * 2, SEQ, D)
```

```python
from contextlib import ExitStack

import concourse.bass as bass
from concourse import mybir

F32 = mybir.dt.float32
BF16 = mybir.dt.bfloat16
I32 = mybir.dt.int32
U32 = mybir.dt.uint32
ALU = mybir.AluOpType
ACT = mybir.ActivationFunctionType
AX = mybir.AxisListType

P = 128
TOKENS, D = 512, 192
TILES = TOKENS // P
SEQ = 64
FEAT = 768
KT = FEAT // P
HEADS, HD = 12, 16
D0, D1 = 128, 64
H0, H1 = D0 // HD, D1 // HD
HP = HEADS // 2
VC = 2 * (HD + 1)
E, HID, BOT = 32, 512, 64
HT = HID // P
UNITS = E // 2
CAP = 64
EXTRA = 2 * TOKENS // CAP
NOWHERE = float(1 << 20)
RING = 4
W1C, W2C, W3C = 3 * HID, 2 * HT * HID, 2 * HT * BOT
MID = W1C
HI = W1C + W2C
WC = HI + W3C + D
EPS = 1e-5

WARM_1, WARM_2 = 22, 12
LAG = 3.0
(AT_LN1, AT_XNT, AT_QKV, AT_BIAS, AT_ROPE, AT_QKT, AT_SCORES, AT_SOFT, AT_PT, AT_VALUES, AT_ATT,
 AT_PROJECT, AT_LN2, AT_X2T, AT_GATE, AT_CHOOSE, AT_RANK, AT_SLOT) = (
    2.5, 5, 6, 8.5, 9.5, 12, 15, 16.5, 19, 21, 23, 26, 28, 30, 32, 33, 35, 36)

C_ID, C_TRI, C_CAUS, C_COS, C_SIN, C_M0, C_M1, C_IOTA, C_PAIR = range(9)
C_COLS = [P, P, SEQ, 2 * HD, 2 * HD, H0, H1, E, UNITS]
C_AT = [sum(C_COLS[:i]) for i in range(len(C_COLS) + 1)]
NC_ = C_AT[-1]


def vit_layer(nc, xp_d, wt_d, wqk_d, wv_d, wo_d, gate_d, rows_d, bv_d, consts_d, experts_d,
              b12_d, b3_d, bl_d, out_d):
    slots_d = nc.dram_tensor("slots_d", ((UNITS + EXTRA) * P, D), F32, kind="Internal").ap()
    results_d = nc.dram_tensor("results_d", ((UNITS + EXTRA) * P, D), F32, kind="Internal").ap()
    ctx = ExitStack()
    with ctx:
        def sb(name, shape, dt=F32):
            return ctx.enter_context(nc.sbuf_tensor(name, shape, dt))

        def sem(name):
            return ctx.enter_context(nc.semaphore(name))

        ring = sb("ring", [P, RING, WC])
        cst = sb("cst", [P, NC_])

        def const(i):
            return cst[:, C_AT[i]:C_AT[i + 1]]
        ident = const(C_ID)
        xp = sb("xp", [P, TILES, KT * P])
        wt = sb("wt", [P, KT, D])
        wqk0, wqk1 = sb("wqk0", [P, 2 * D]), sb("wqk1", [D1, 2 * D])
        wv0, wv1 = sb("wv0", [P, D]), sb("wv1", [D1, D])
        wo0, wo1 = sb("wo0", [P, D]), sb("wo1", [D1, D])
        g0, g1 = sb("g0", [P, E]), sb("g1", [D1, E])
        rows = sb("rows", [P, 4 * D])
        bv = sb("bv", [P, HP * HD])
        b12 = sb("b12", [P, UNITS, 2, HT * 2])
        b3 = sb("b3", [P, UNITS])
        bl = sb("bl", [E, D])
        identb = sb("identb", [P, P], BF16)
        causb = sb("causb", [P, H0, SEQ], BF16)
        trib = sb("trib", [P, P], BF16)
        onesb = sb("onesb", [P, P], BF16)
        halfneg = sb("halfneg", [P, 1])

        h = sb("h", [P, TILES, D])
        stats = sb("stats", [P, TILES, 6])
        mv = sb("mv", [P, TILES, 2])
        rstd = sb("rstd", [P, TILES])
        xn = sb("xn", [P, 2, D])
        xnT = sb("xnT", [P, 2, 2, P])
        qk_area = sb("qk_area", [P, 4, 2 * D])
        qkb, rcos = qk_area[:, 0:2], qk_area[:, 2:4]
        rsin = sb("rsin", [P, 2 * D])
        rot = sb("rot", [P, 2, 2 * D])
        qT = sb("qT", [P, 2, 2, P])
        kx0 = sb("kx0", [P, 2, 2, H0 * SEQ])
        kx1 = sb("kx1", [P, 2, 2, H1 * SEQ])
        vbd = sb("vbd", [P, TILES, 2, HP * VC])
        smax = sb("smax", [P, 2, HEADS])
        ssub = sb("ssub", [P, HEADS * SEQ])
        prob = sb("prob", [P, 2, HEADS * SEQ])
        pT = sb("pT", [P, 2, HP * P])
        rden = sb("rden", [P, 2, HEADS])
        att = sb("att", [P, 2, D])
        attT = sb("attT", [P, 2, 2, P])
        h2 = sb("h2", [P, TILES, D])
        xn2 = sb("xn2", [P, TILES, D])
        xn2T = sb("xn2T", [P, 2, 2, P])
        lg = sb("lg", [P, TILES, E])
        s4 = sb("s4", [P, 8, TILES])
        top = sb("top", [P, TILES, 8])
        topi = sb("topi", [P, TILES, 8], U32)
        topf = sb("topf", [P, TILES, 2])
        oh = sb("oh", [P, TILES, 2, E])
        ohb = sb("ohb", [P, TILES, E], BF16)
        rtmp = kx0[:].rearrange("p a i n -> p (a i n)")
        ohr = rtmp[:, 0:TILES * 2 * E].rearrange("p (t k e) -> p t k e", t=TILES, k=2)
        gs, ge, prb, wd = (rtmp[:, i * P:(i + 1) * P].rearrange("p (t e) -> p t e", e=E) for i in range(2, 6))
        rank2 = sb("rank2", [P, TILES, 2])
        slot2 = sb("slot2", [P, 5, TILES, 2])
        rounds = sb("rounds", [P, TILES, 2], I32)
        first_sl = sb("first_sl", [P, TILES, 2], I32)
        spill_sl = sb("spill_sl", [P, TILES, 2], I32)
        sl = sb("sl", [P, TILES, 2], I32)
        w12 = sb("w12", [P, 2, TILES])
        cnti = sb("cnti", [P, E], I32)
        xtra = sb("xtra", [P, 6, UNITS])
        bext = sb("bext", [P, E])
        xcount = sb("xcount", [1, EXTRA])
        xlist = sb("xlist", [1, EXTRA + 1], I32)
        y0 = prob[:, 0, :].rearrange("p (t d) -> p t d", t=TILES)
        wdT = prob[0:E, 1, 0:TILES * P].rearrange("p (t n) -> p t n", t=TILES)
        xtab = prob[0:1, 1, TILES * P:TILES * P + EXTRA * UNITS].rearrange("p (j u) -> p j u", j=EXTRA)
        blank = sb("blank", [P, D])

        xs = kx1[:].rearrange("p a i n -> p (a i n)")[:, 0:RING * D].rearrange("p (s c) -> p s c", s=RING)
        after_wt = wt[:].rearrange("p k d -> p (k d)")
        xm = after_wt[:, 0:2 * P].rearrange("p (b s) -> p b s", b=2)
        ob = after_wt[:, 2 * P:2 * P + RING * D].rearrange("p (b d) -> p b d", b=RING)
        picked = qk_area[:].rearrange("p t (k d) -> p t k d", k=2)
        xt = sb("xt", [P, 2, P])
        pre1, pre2, hb1, hb2, h1T_, h2Ta = (
            xp[:].rearrange("p t k -> p (t k)")[:, i * HID:(i + 1) * HID] for i in range(6))
        h2Tb = sb("h2Tb", [P, HID])
        h2T_ = (h2Ta, h2Tb[:])
        h1T, *h2T = (v.rearrange("p (k s) -> p k s", k=HT) for v in (h1T_, *h2T_))
        zbd = sb("zbd", [P, P])
        held = sb("held", [1, 1])

        bank = [ctx.enter_context(nc.psum_tensor(f"bank{i}", [P, 512], F32)) for i in range(8)]

        s_xp = [sem(f"s_xp{t}") for t in range(TILES)]
        s_wt, s_cst, s_rows, s_wqkv, s_late = map(sem, ("s_wt", "s_cst", "s_rows", "s_wqkv", "s_late"))
        s_lo = [sem(f"s_lo{i}") for i in range(RING)]
        s_mid = [sem(f"s_mid{i}") for i in range(RING)]
        s_hi = [sem(f"s_hi{i}") for i in range(RING)]
        s_set = sem("s_set")
        s_cast = sem("s_cast")
        s_v = sem("s_v")
        s_blank, s_scat, s_spill, s_out = map(sem, ("s_blank", "s_scat", "s_spill", "s_out"))
        s_xs = [sem(f"s_xs{i}") for i in range(RING)]
        (embedded, h_done, st1, rs1, xn_done, xnt_ps, xnt_done, qk_ps, v_ps, qkb_done, cos_done, v_done,
         rot_done, qt_ps, kt_ps, qt_done, kx1_done, kx0_done, sc_ps, sub_done, exp_done, pt_ps, pt_done,
         pv_ps, att_done, at_ps, at_done, wo_ps, hbo_done, st2, rs2, xn2_done, x2_ps, x2_done,
         lg_ps, lg_done, out_done) = (sem(n) for n in (
             "embedded h_done st1 rs1 xn_done xnt_ps xnt_done qk_ps v_ps qkb_done cos_done v_done "
             "rot_done qt_ps kt_ps qt_done kx1_done kx0_done sc_ps sub_done exp_done pt_ps pt_done "
             "pv_ps att_done at_ps at_done wo_ps hbo_done st2 rs2 xn2_done x2_ps x2_done "
             "lg_ps lg_done out_done").split())
        gsub, gexp, oh_done, rank_ps, rank_read, first_done, slot_done, xlist_done, wd_done, wdt_ps, wdt_done, bl_ps, y0_done = (
            sem(n) for n in ("gsub gexp oh_done rank_ps rank_read first_done slot_done xlist_done wd_done wdt_ps wdt_done "
                             "bl_ps y0_done").split())
        (x_ps, x_done, l1_ps, c1_done, ta_ps, a1_done, g1_done, l2_ps, c2_done, tb_ps, a2_done, g2_done,
         l3_ps, z_done, o_ps, o_done) = (sem(n) for n in (
             "x_ps x_done l1_ps c1_done ta_ps a1_done g1_done l2_ps c2_done tb_ps a2_done g2_done "
             "l3_ps z_done o_ps o_done").split())
        s_ob = [sem(f"s_ob{i}") for i in range(RING)]
        s_pick = [sem(f"s_pick{t}") for t in range(TILES)]
        s_pool = sem("s_pool")

        block = ctx.enter_context(nc.Block())

        def in_order(stages):
            return [(fn, t) for _, t, fn in sorted(((t * LAG + at, t, fn) for fn, at in stages for t in range(TILES)),
                                                   key=lambda x: x[:2])]

        def unit_at(g, k):
            return g * RING + k, k % RING, g + k // RING

        TURNS = 2
        LOOP_END = 2 + TURNS * RING
        BRANCH = UNITS - 3

        @block.sync
        def _(sp):
            def load_lo(pair, s):
                sp.dma_start(ring[:, s, 0:MID], experts_d[pair, :, 0:MID]).then_inc(s_lo[s], 16)

            def load_mid(pair, s):
                sp.dma_start(ring[:, s, MID:HI], experts_d[pair, :, MID:HI]).then_inc(s_mid[s], 16)

            def load_hi(pair, s):
                sp.dma_start(ring[:, s, HI:WC], experts_d[pair, :, HI:WC]).then_inc(s_hi[s], 16)

            def load_rows(unit_, s):
                sp.dma_start(xs[:, s, :], by_unit[:, bass.ds(unit_, 1), :].rearrange("p u c -> p (u c)"))\
                    .then_inc(s_xs[s], 16)

            by_unit = slots_d.rearrange("(u p) c -> p u c", p=P)
            sp.dma_start(xp[:, 0, :], xp_d[0]).then_inc(s_xp[0], 16)
            sp.dma_start(wt[:], wt_d).then_inc(s_wt, 16)
            sp.dma_start(cst[:], consts_d).then_inc(s_cst, 16)
            sp.dma_start(rows[:], rows_d.partition_broadcast(P)).then_inc(s_rows, 16)
            sp.dma_start(xp[:, 1, :], xp_d[1]).then_inc(s_xp[1], 16)
            sp.dma_start(wqk0[:], wqk_d[0:D0]).then_inc(s_wqkv, 16)
            sp.dma_start(wqk1[:], wqk_d[D0:D]).then_inc(s_wqkv, 16)
            sp.dma_start(wv0[:], wv_d[0:D0]).then_inc(s_wqkv, 16)
            sp.dma_start(wv1[:], wv_d[D0:D]).then_inc(s_wqkv, 16)
            for half in range(2):
                sp.dma_start(bv[64 * half:64 * half + 64, :],
                             bv_d[half].partition_broadcast(64)).then_inc(s_wqkv, 16)
            for t in range(2, TILES):
                sp.dma_start(xp[:, t, :], xp_d[t]).then_inc(s_xp[t], 16)
            for dst, src in ((wo0[:], wo_d[0:D0]), (wo1[:], wo_d[D0:D]), (g0[:], gate_d[0:D0]),
                             (g1[:], gate_d[D0:D]), (b12[:], b12_d), (b3[:], b3_d), (bl[:], bl_d)):
                sp.dma_start(dst, src).then_inc(s_late, 16)
            for u in range(RING):
                load_lo(u, u)
                load_mid(u, u)
                load_hi(u, u)
                if u == 1:
                    sp.wait_ge(s_set, 10)
                    zeros = blank[:].unsqueeze(1).to_broadcast([P, UNITS, D])
                    sp.dma_start(by_unit[:, 0:UNITS, :], zeros).then_inc(s_blank, 16)
            sp.dma_start(by_unit[:, UNITS:UNITS + EXTRA, :], zeros).then_inc(s_blank, 16)
            sp.dma_start(results_d.rearrange("(u p) c -> p u c", p=P)[:, UNITS:UNITS + EXTRA, :], zeros)\
                .then_inc(s_blank, 16)
            sp.wait_ge(s_scat, 16 * 2 * TILES)
            for u in range(RING):
                load_rows(u, u)

            def store(unit_, s):
                sp.dma_start(results_d.rearrange("(u p) c -> p u c", p=P)[:, bass.ds(unit_, 1), :]
                             .rearrange("p u c -> p (u c)"), ob[:, s, :]).then_inc(s_ob[s], 16)

            def step(g, k, loads, pair=None):
                u = g * RING + k

                def has(ahead):
                    return loads is None or k + ahead < loads

                def whose(ahead):
                    return pair if pair is not None and k + ahead == UNITS else u + ahead
                if k >= 2:
                    sp.wait_ge(o_done, u - 1)
                    store(u - 2, (k - 2) % RING)
                    if has(2):
                        load_hi(whose(2), (k + 2) % RING)
                if has(4):
                    if k < 2:
                        sp.wait_ge(l2_ps, u + 1)
                    load_mid(whose(4), k % RING)
                if has(6):
                    sp.wait_ge(l1_ps, u + 3)
                    load_rows(u + 6, (k + 2) % RING)
                    load_lo(whose(6), (k + 2) % RING)

            for u in (4, 5):
                sp.wait_ge(l1_ps, u - RING + 1)
                load_rows(u, u - RING)
                load_lo(u, u - RING)
            for k in range(2):
                step(0, k, UNITS)
            with sp.Fori(0, TURNS) as g:
                for k in range(2, 2 + RING):
                    step(g, k, None)
            sp.wait_ge(xlist_done, 1)
            extra = sp.value_load(xlist[0:1, EXTRA:EXTRA + 1], min_val=0, max_val=EXTRA)
            with sp.If(extra > 0):
                pair = sp.value_load(xlist[0:1, 0:1], min_val=0, max_val=UNITS - 1)
                sp.wait_ge(s_spill, 16 * 2 * TILES)
                for k in range(LOOP_END, UNITS + 3):
                    step(0, k, UNITS + 1, pair)
            with sp.If(extra < 1):
                for k in range(LOOP_END, UNITS + 2):
                    step(0, k, UNITS)
            with sp.If(extra > 1):
                with sp.Fori(1, extra) as j:
                    pair = sp.value_load(xlist[0:1, bass.ds(j, 1)], min_val=0, max_val=UNITS - 1)
                    load_rows(j + UNITS, 0)
                    load_lo(pair, 0)
                    load_mid(pair, 0)
                    load_hi(pair, 0)
                    sp.wait_ge(o_done, j + (UNITS + 1))
                    store(j + UNITS, 0)
            for t in range(TILES):
                sp.wait_ge(out_done, t + 1)
                sp.dma_start(out_d.rearrange("(t p) d -> p t d", p=P)[:, t, :], y0[:, t, :]).then_inc(s_out, 16)
            sp.wait_ge(s_out, 16 * TILES)

        @block.gpsimd
        def _(pool):
            finished = []

            def done(ins, signal):
                ins.then_inc(signal, 1)
                finished.append(signal)
                pool.wait_ge(signal, finished.count(signal))

            done(pool.memset(blank[:], 0.0), s_set)
            done(pool.memset(vbd[:], 0.0), s_set)
            vr = vbd[:].rearrange("p t i (c v) -> p (t i c) v", v=VC)
            done(pool.memset(vr[0:64, :, HD:HD + 1], 1.0), s_set)
            done(pool.memset(vr[64:P, :, VC - 1:VC], 1.0), s_set)
            done(pool.memset(halfneg[:], -0.5), s_set)
            done(pool.memset(qT[D1:P, :, 1, :], 0.0), s_set)
            done(pool.memset(kx1[D1:P], 0.0), s_set)
            done(pool.memset(onesb[:], 1.0), s_set)
            done(pool.memset(xt[:], 0.0), s_set)
            done(pool.memset(zbd[:], 0.0), s_set)
            for s in range(RING):
                done(pool.memset(held[:], 0.0), s_ob[s])

            def inverse_root(t, stat, ready):
                pool.wait_ge(stat, t + 1)
                done(pool.tensor_scalar(rstd[:, t:t + 1], mv[:, t, 1:2], EPS, None, ALU.add), s_pool)
                done(pool.tensor_tensor(rstd[:, t:t + 1], rstd[:, t:t + 1], halfneg[:], ALU.pow), ready)

            def ln1(t):
                inverse_root(t, st1, rs1)

            def rope_cos(t):
                pool.wait_ge(qkb_done, t + 1)
                if t >= 2:
                    pool.wait_ge(rot_done, t - 1)
                done(pool.tensor_tensor(rcos[:, t % 2, :].rearrange("p (a n d) -> p a n d", a=2, d=HD),
                                   qkb[:, t % 2, :].rearrange("p (a n d) -> p a n d", a=2, d=HD),
                                   const(C_COS).rearrange("p (a d) -> p a d", a=2).unsqueeze(2)
                                   .to_broadcast([P, 2, HEADS, HD]), ALU.mult), cos_done)

            def hbo_add(t):
                pool.wait_ge(xn_done, t + 1)
                done(pool.tensor_tensor(h[:, t, :], h[:, t, :], rows[:, 3 * D:4 * D], ALU.add), hbo_done)

            def ln2(t):
                inverse_root(t, st2, rs2)

            def dispatch(t):
                pool.wait_ge(first_done, t + 1)
                pool.wait_ge(xn2_done, t + 1)
                if t == 0:
                    pool.wait_ge(s_blank, 48)
                for k in range(2):
                    pool.indirect_dma_start(slots_d, bass.IndirectOffsetOnAxis(ap=first_sl[:, t, k:k + 1], axis=0),
                                            xn2[:, t, :], None, bounds_check=UNITS * P - 1, oob_is_err=False)\
                        .then_inc(s_scat, 16)

            pool.wait_ge(s_rows, 16)
            pool.wait_ge(s_cst, 16)
            for stage, t in in_order([(ln1, AT_LN1), (rope_cos, AT_ROPE), (hbo_add, AT_ROPE + 1), (ln2, AT_LN2),
                                      (dispatch, AT_SLOT)]):
                stage(t)

            pool.wait_ge(xlist_done, 1)
            extra = pool.value_load(xlist[0:1, EXTRA:EXTRA + 1], min_val=0, max_val=EXTRA)
            with pool.If(extra > 0):
                for t in range(TILES):
                    for k in range(2):
                        pool.indirect_dma_start(slots_d, bass.IndirectOffsetOnAxis(ap=spill_sl[:, t, k:k + 1], axis=0),
                                                xn2[:, t, :], None, bounds_check=(UNITS + EXTRA) * P - 1,
                                                oob_is_err=False).then_inc(s_spill, 16)
            for s in range(1, RING):
                pool.wait_ge(s_ob[s], 1 + 16 * (UNITS // RING))
            pool.wait_ge(s_ob[0], extra * 16 + (1 + 16 * (UNITS // RING)))
            pool.tensor_tensor(held[:], halfneg[0:1, :], halfneg[0:1, :], ALU.add).then_inc(s_pool, 1)
            for t in range(TILES):
                for k in range(2):
                    pool.indirect_dma_start(picked[:, t, k, :], None, results_d,
                                            bass.IndirectOffsetOnAxis(ap=sl[:, t, k:k + 1], axis=0))\
                        .then_inc(s_pick[t], 16)

        @block.scalar
        def _(act):
            act.wait_ge(s_cst, 16)
            act.activation(identb[:], ident, ACT.Copy)
            act.activation(trib[:], const(C_TRI), ACT.Copy)
            act.activation(causb[:], const(C_CAUS).unsqueeze(1).to_broadcast([P, H0, SEQ]),
                           ACT.Copy).then_inc(s_cast, 1)
            act.wait_ge(s_set, 10)

            def copies(dst, src_bank, t, ready, done):
                act.wait_ge(ready, t + 1)
                act.activation(dst[:, t % 2, 0, :], src_bank[:, 0:P], ACT.Copy)
                act.activation(dst[0:D1, t % 2, 1, :], src_bank[0:D1, P:2 * P], ACT.Copy).then_inc(done, 1)

            def xn_t(t):
                if t >= 2:
                    act.wait_ge(v_ps, t - 1)
                copies(xnT, bank[2], t, xnt_ps, xnt_done)

            def q_t(t):
                if t >= 2:
                    act.wait_ge(sc_ps, t - 1)
                copies(qT, bank[6], t, qt_ps, qt_done)
                for n in range(H1):
                    last = act.activation(
                        kx1[0:D1, t % 2].rearrange("p i (n s) -> p i n s", s=SEQ)[:, :, n, :],
                        bank[6][0:D1, 2 * P:3 * P].rearrange("p (i s) -> p i s", s=SEQ),
                        ACT.Copy, scale=const(C_M1)[0:D1, n:n + 1])
                last.then_inc(kx1_done, 1)

            def exp_s(t):
                if t >= 2:
                    act.wait_ge(pt_ps, t - 1)
                act.wait_ge(sub_done, t + 1)
                act.activation(prob[:, t % 2, :], ssub[:], ACT.Exp).then_inc(exp_done, 1)

            def p_t(t):
                if t >= 2:
                    act.wait_ge(pv_ps, t - 1)
                act.wait_ge(pt_ps, t + 1)
                act.activation(pT[:, t % 2, 0:4 * P], bank[2][:], ACT.Copy)
                act.activation(pT[:, t % 2, 4 * P:6 * P], bank[3][:, 0:2 * P], ACT.Copy).then_inc(pt_done, 1)

            def att_t(t):
                if t >= 2:
                    act.wait_ge(wo_ps, t - 1)
                copies(attT, bank[6], t, at_ps, at_done)

            def xn2_t(t):
                if t >= 2:
                    act.wait_ge(lg_ps, t - 1)
                copies(xn2T, bank[2], t, x2_ps, x2_done)

            for stage, t in in_order([(xn_t, AT_XNT), (q_t, AT_QKT), (exp_s, AT_SOFT), (p_t, AT_PT),
                                      (att_t, AT_ATT), (xn2_t, AT_X2T)]):
                stage(t)

            def copy_1(u):
                act.wait_ge(l1_ps, u + 1)
                act.activation(pre1[:], bank[1][:], ACT.Copy).then_inc(c1_done, 1)

            def copy_2(u):
                act.wait_ge(l2_ps, u + 1)
                act.activation(pre2[:], bank[2][:], ACT.Copy).then_inc(c2_done, 1)

            def gelu_1(u):
                act.wait_ge(a1_done, u + 1)
                act.activation(h1T_, hb1[:], ACT.Gelu).then_inc(g1_done, 1)

            def gelu_2(u, b):
                act.wait_ge(a2_done, u + 1)
                act.activation(h2T_[b], hb2[:], ACT.Gelu).then_inc(g2_done, 1)

            def step(u, b, ahead=2):
                copy_2(u)
                if ahead >= 1:
                    gelu_1(u + 1)
                if ahead >= 2:
                    copy_1(u + 2)
                gelu_2(u, b)

            act.wait_ge(gsub, 1)
            act.activation(ge, gs, ACT.Exp).then_inc(gexp, 1)
            copy_1(0)
            gelu_1(0)
            copy_1(1)
            with act.Fori(0, UNITS // 2 - 1) as g:
                for b in range(2):
                    step(g * 2 + b, b)
            act.wait_ge(xlist_done, 1)
            extra = act.value_load(xlist[0:1, EXTRA:EXTRA + 1], min_val=0, max_val=EXTRA)
            with act.If(extra < 1):
                step(UNITS - 2, 0, 1)
                step(UNITS - 1, 1, 0)
            with act.If(extra > 0):
                step(UNITS - 2, 0, 2)
                step(UNITS - 1, 1, 1)
                step(UNITS, 0, 0)
            with act.If(extra > 1):
                with act.Fori(1, extra) as j:
                    copy_1(j + UNITS)
                    gelu_1(j + UNITS)
                    copy_2(j + UNITS)
                    gelu_2(j + UNITS, 0)

        @block.vector
        def _(dve):
            chain = [0]

            def link(ins):
                chain[0] += 1
                ins.then_inc(s_v, 1)
                dve.wait_ge(s_v, chain[0])

            def ln1_a(t):
                dve.wait_ge(embedded, t + 1)
                ins = dve.tensor_tensor(h[:, t, :], bank[t % 2][:, 0:D], rows[:, 0:D], ALU.add)
                ins.then_inc(h_done, 1)
                dve.wait_ge(h_done, t + 1)
                link(dve.bn_stats(stats[:, t, :], h[:, t, :]))
                dve.bn_aggr(mv[:, t, :], stats[:, t, :]).then_inc(st1, 1)

            def ln1_b(t):
                dve.wait_ge(rs1, t + 1)
                if t >= 2:
                    dve.wait_ge(xnt_ps, t - 1)
                dve.wait_ge(st1, t + 1)
                dve.tensor_scalar(xn[:, t % 2, :], h[:, t, :], mv[:, t, 0:1], rstd[:, t:t + 1],
                                  ALU.subtract, ALU.mult).then_inc(xn_done, 1)

            def qkv(t):
                dve.wait_ge(qk_ps, t + 1)
                if t >= 2:
                    dve.wait_ge(cos_done, t - 1)
                dve.tensor_tensor(qkb[:, t % 2, :], bank[4][:, 0:2 * D], rows[:, D:3 * D], ALU.add)\
                    .then_inc(qkb_done, 1)
                dve.wait_ge(v_ps, t + 1)
                for half in range(2):
                    q = slice(64 * half, 64 * half + 64)
                    c = (HD + 1) * half
                    last = dve.tensor_tensor(
                        vbd[q, t].rearrange("p i (c v) -> p i c v", v=VC)[:, :, :, c:c + HD],
                        bank[5][q, 0:2 * HP * HD].rearrange("p (i c d) -> p i c d", i=2, d=HD),
                        bv[q, :].rearrange("p (c d) -> p c d", d=HD).unsqueeze(1)
                        .to_broadcast([64, 2, HP, HD]), ALU.add)
                last.then_inc(v_done, 1)

            def rope(t):
                dve.wait_ge(qkb_done, t + 1)
                half_ = HD // 2
                src = qkb[:, t % 2, :].rearrange("p (a n d) -> p a n d", a=2, d=HD)
                dst = rsin[:].rearrange("p (a n d) -> p a n d", a=2, d=HD)
                sin = const(C_SIN).rearrange("p (a d) -> p a d", a=2).unsqueeze(2)\
                    .to_broadcast([P, 2, HEADS, HD])
                if t >= 1:
                    dve.wait_ge(rot_done, t)
                dve.tensor_tensor(dst[:, :, :, 0:half_], src[:, :, :, half_:HD], sin[:, :, :, 0:half_], ALU.mult)
                link(dve.tensor_tensor(dst[:, :, :, half_:HD], src[:, :, :, 0:half_], sin[:, :, :, half_:HD],
                                       ALU.mult))
                dve.wait_ge(cos_done, t + 1)
                if t >= 2:
                    dve.wait_ge(kt_ps, t - 1)
                dve.tensor_tensor(rot[:, t % 2, :], rcos[:, t % 2, :], rsin[:], ALU.add).then_inc(rot_done, 1)

            def keys(t):
                dve.wait_ge(kt_ps, t + 1)
                if t >= 2:
                    dve.wait_ge(sc_ps, t - 1)
                for i in range(2):
                    last = dve.tensor_tensor(
                        kx0[:, t % 2, i, :].rearrange("p (n s) -> p n s", s=SEQ),
                        bank[7][:, i * SEQ:(i + 1) * SEQ].unsqueeze(1).to_broadcast([P, H0, SEQ]),
                        const(C_M0).unsqueeze(2).to_broadcast([P, H0, SEQ]), ALU.mult)
                last.then_inc(kx0_done, 1)

            def scores(t):
                dve.wait_ge(sc_ps, t + 1)
                m = smax[:, t % 2, :]
                s0 = bank[0][:].rearrange("p (n s) -> p n s", s=SEQ)
                s1 = bank[1][:, 0:H1 * SEQ].rearrange("p (n s) -> p n s", s=SEQ)
                dve.tensor_reduce(m[:, 0:H0], s0, AX.X, ALU.max)
                link(dve.tensor_reduce(m[:, H0:HEADS], s1, AX.X, ALU.max))
                if t >= 1:
                    dve.wait_ge(exp_done, t)
                out = ssub[:].rearrange("p (n s) -> p n s", s=SEQ)
                dve.tensor_tensor(out[:, 0:H0, :], s0, m[:, 0:H0].unsqueeze(2).to_broadcast([P, H0, SEQ]), ALU.subtract)
                dve.tensor_tensor(out[:, H0:HEADS, :], s1, m[:, H0:HEADS].unsqueeze(2).to_broadcast([P, H1, SEQ]),
                                  ALU.subtract).then_inc(sub_done, 1)

            def attend(t):
                dve.wait_ge(pv_ps, t + 1)
                pv = bank[4][:, 0:HP * VC].rearrange("p (n v) -> p n v", v=HD + 1)
                if t >= 2:
                    dve.wait_ge(at_ps, t - 1)
                link(dve.reciprocal(rden[:, t % 2, :], pv[:, :, HD]))
                dve.tensor_tensor(att[:, t % 2, :].rearrange("p (n d) -> p n d", d=HD), pv[:, :, 0:HD],
                                  rden[:, t % 2, :].unsqueeze(2).to_broadcast([P, HEADS, HD]), ALU.mult)\
                    .then_inc(att_done, 1)

            def ln2_a(t):
                dve.wait_ge(wo_ps, t + 1)
                dve.wait_ge(hbo_done, t + 1)
                link(dve.tensor_tensor(h2[:, t, :], bank[0][:, 0:D], h[:, t, :], ALU.add))
                link(dve.bn_stats(stats[:, t, :], h2[:, t, :]))
                dve.bn_aggr(mv[:, t, :], stats[:, t, :]).then_inc(st2, 1)

            def ln2_b(t):
                dve.wait_ge(rs2, t + 1)
                dve.wait_ge(st2, t + 1)
                dve.tensor_scalar(xn2[:, t, :], h2[:, t, :], mv[:, t, 0:1], rstd[:, t:t + 1],
                                  ALU.subtract, ALU.mult).then_inc(xn2_done, 1)

            iota = const(C_IOTA)

            def choose(t):
                dve.wait_ge(lg_ps, t + 1)
                dve.tensor_copy(lg[:, t, :], bank[5][:, 0:E]).then_inc(lg_done, 1)
                dve.wait_ge(lg_done, t + 1)
                link(dve.max(top[:, t, :], lg[:, t, :]))
                link(dve.max_index(topi[:, t, :], top[:, t, :], lg[:, t, :]))
                link(dve.tensor_copy(topf[:, t, :], topi[:, t, 0:2]))
                link(dve.tensor_tensor(oh[:, t], iota.unsqueeze(1).to_broadcast([P, 2, E]),
                                       topf[:, t, :].unsqueeze(2).to_broadcast([P, 2, E]), ALU.is_equal))
                dve.tensor_tensor(ohb[:, t, :], oh[:, t, 0, :], oh[:, t, 1, :], ALU.add).then_inc(oh_done, 1)

            def place(t):
                dve.wait_ge(rank_ps, t + 1)
                if t == 0:
                    dve.wait_ge(sc_ps, TILES)
                dve.tensor_tensor(ohr[:, t], bank[7][:, 0:E].unsqueeze(1).to_broadcast([P, 2, E]),
                                  oh[:, t], ALU.mult).then_inc(rank_read, 1)
                dve.wait_ge(rank_read, t + 1)
                link(dve.tensor_reduce(rank2[:, t, :], ohr[:, t], AX.X, ALU.add))
                dve.tensor_scalar(slot2[:, 0, t, :], rank2[:, t, :], float(CAP), NOWHERE, ALU.is_ge, ALU.mult)
                link(dve.scalar_tensor_tensor(slot2[:, 1, t, :], topf[:, t, :], float(CAP), rank2[:, t, :],
                                              ALU.mult, ALU.add))
                dve.tensor_tensor(first_sl[:, t, :], slot2[:, 0, t, :], slot2[:, 1, t, :], ALU.add)\
                    .then_inc(first_done, 1)

            dve.wait_ge(s_rows, 16)
            dve.wait_ge(s_cst, 16)
            dve.wait_ge(s_set, 10)
            dve.wait_ge(s_wqkv, 96)
            for stage, t in in_order([(ln1_a, AT_LN1), (ln1_b, AT_XNT - 0.5), (qkv, AT_BIAS), (rope, AT_ROPE),
                                      (keys, AT_QKT), (scores, AT_SOFT), (attend, AT_ATT - 0.5), (ln2_a, AT_LN2),
                                      (ln2_b, AT_X2T - 0.5), (choose, AT_CHOOSE), (place, AT_SLOT)]):
                stage(t)

            wide, both = [P, TILES, E], [P, TILES, 2, E]
            dve.tensor_tensor(gs, lg[:], top[:, :, 0:1].to_broadcast(wide), ALU.subtract).then_inc(gsub, 1)
            dve.wait_ge(rank_ps, TILES + 1)
            link(dve.tensor_scalar(cnti[:], bank[4][:, 0:E], float(CAP - 1), None, ALU.add))
            link(dve.tensor_scalar(cnti[:], cnti[:], 6, None, ALU.logical_shift_right))
            pairs = cnti[:].rearrange("p (u e) -> p u e", e=2)
            a, b, base, incl = (xtra[:, i, :] for i in range(4))
            link(dve.tensor_tensor(a, pairs[:, :, 0], pairs[:, :, 1], ALU.max))
            link(dve.tensor_scalar(a, a, 1.0, -1.0, ALU.max, ALU.add))
            src, dst, shift = a, b, 1
            while shift < UNITS:
                dve.tensor_copy(dst[:, 0:shift], src[:, 0:shift])
                link(dve.tensor_tensor(dst[:, shift:UNITS], src[:, shift:UNITS], src[:, 0:UNITS - shift], ALU.add))
                src, dst, shift = dst, (incl if dst is b else b), shift * 2
            incl_ = src
            link(dve.tensor_tensor(xtab, incl_[0:1, :].unsqueeze(1).to_broadcast([1, EXTRA, UNITS]),
                                   iota[0:1, 0:EXTRA].unsqueeze(2).to_broadcast([1, EXTRA, UNITS]), ALU.is_le))
            link(dve.tensor_reduce(xcount[:], xtab, AX.X, ALU.add))
            link(dve.tensor_scalar(xcount[:], xcount[:], float(UNITS - 1), None, ALU.min))
            dve.tensor_copy(xlist[:, 0:EXTRA], xcount[:])
            link(dve.tensor_copy(xlist[:, EXTRA:EXTRA + 1], incl_[0:1, UNITS - 1:UNITS]))
            base = xtra[:, 4, :]
            dve.memset(base[:, 0:1], 0.0)
            link(dve.tensor_copy(base[:, 1:UNITS], incl_[:, 0:UNITS - 1]))
            link(dve.tensor_tensor(base, base, const(C_PAIR), ALU.subtract))
            for e in range(2):
                last = dve.tensor_scalar(bext[:].rearrange("p (u e) -> p u e", e=2)[:, :, e], base,
                                         float(UNITS - 1), float(P), ALU.add, ALU.mult)
            link(last)
            beyond, plain, jump, round_, away = (slot2[:, i] for i in range(5))
            dve.tensor_copy(rounds[:], rank2[:])
            link(dve.tensor_tensor(ohr, bext[:].unsqueeze(1).unsqueeze(1).to_broadcast(both), oh[:], ALU.mult))
            dve.tensor_scalar(rounds[:], rounds[:], 6, 6, ALU.logical_shift_right, ALU.logical_shift_left)
            dve.tensor_scalar(beyond, rank2[:], float(CAP), None, ALU.is_ge)
            link(dve.tensor_reduce(jump, ohr, AX.X, ALU.add))
            link(dve.tensor_tensor(round_, rounds[:], jump, ALU.add))
            dve.tensor_scalar(away, beyond, -NOWHERE, NOWHERE, ALU.mult, ALU.add)
            link(dve.tensor_tensor(round_, round_, beyond, ALU.mult))
            link(dve.tensor_tensor(plain, plain, round_, ALU.add))
            dve.tensor_copy(sl[:], plain)
            dve.tensor_tensor(spill_sl[:], plain, away, ALU.add).then_inc(xlist_done, 1)
            def rows_in(u, b):
                dve.wait_ge(x_ps, u + 1)
                dve.tensor_copy(xm[:, b, :], bank[0][:, 64:64 + P])
                dve.tensor_copy(xt[0:64, b, 0:64], bank[0][0:64, 0:64])
                dve.tensor_copy(xt[64:P, b, 64:P], bank[0][64:P, P + 64:2 * P]).then_inc(x_done, 1)

            def add_bias(u, pair, k, out, bank_, ready, done):
                dve.wait_ge(ready, u + 1)
                dve.tensor_tensor(out[:].rearrange("p (k s) -> p k s", s=CAP),
                                  bank_[:].rearrange("p (k s) -> p k s", s=CAP),
                                  pair_bias(pair, k).to_broadcast([P, 2 * HT, CAP]), ALU.add).then_inc(done, 1)

            def pair_bias(pair, k):
                return b12[:, bass.ds(pair, 1), k, :].rearrange("p u k -> p (u k)").unsqueeze(2)

            def bottle(u, pair):
                dve.wait_ge(l3_ps, u + 1)
                for half in range(2):
                    q = slice(64 * half, 64 * half + 64)
                    last = dve.tensor_scalar(zbd[q, q], bank[5][q, 0:CAP], b3[q, bass.ds(pair, 1)], None, ALU.add)
                last.then_inc(z_done, 1)

            def results(u, s, sent):
                dve.wait_ge(o_ps, u + 1)
                dve.wait_ge(s_ob[s], sent)
                dve.tensor_copy(ob[:, s, :], bank[6][:, 0:D]).then_inc(o_done, 1)

            def step(g, k, first=0, total=None, pair=None):
                def has(ahead):
                    return total is None or first <= k + ahead < total

                def whose(ahead):
                    return pair if k + ahead == UNITS and pair is not None else g * RING + k + ahead
                u = g * RING + k
                if has(-2):
                    _, s, turn = unit_at(g, k - 2)
                    results(u - 2, s, turn * 16 + 1)
                if has(1):
                    add_bias(u + 1, whose(1), 0, hb1, bank[3], ta_ps, a1_done)
                if has(0):
                    add_bias(u, whose(0), 1, hb2, bank[4], tb_ps, a2_done)
                if has(3):
                    rows_in(u + 3, (k + 3) % 2)
                if has(-1):
                    bottle(u - 1, whose(-1))

            dve.wait_ge(s_late, 16 * 7)
            rows_in(0, 0)
            rows_in(1, 1)
            rows_in(2, 0)
            add_bias(0, 0, 0, hb1, bank[3], ta_ps, a1_done)
            z, rz, den = (s4[:, i, :] for i in range(3))
            dve.wait_ge(gexp, 1)
            link(dve.tensor_reduce(z, ge, AX.X, ALU.add))
            link(dve.reciprocal(rz, z))
            link(dve.tensor_tensor(prb, ge, rz.unsqueeze(2).to_broadcast(wide), ALU.mult))
            link(dve.tensor_tensor(ohr, prb.unsqueeze(2).to_broadcast(both), oh[:], ALU.mult))
            for k in range(2):
                last = dve.tensor_reduce(w12[:, k, :], ohr[:, :, k, :], AX.X, ALU.add)
            link(last)
            link(dve.tensor_tensor(den, w12[:, 0, :], w12[:, 1, :], ALU.add))
            link(dve.tensor_scalar(den, den, 1e-20, None, ALU.add))
            link(dve.reciprocal(rz, den))
            link(dve.tensor_tensor(w12[:], w12[:], rz.unsqueeze(1).to_broadcast([P, 2, TILES]), ALU.mult))
            for k in range(2):
                last = dve.tensor_tensor(ohr[:, :, k, :], oh[:, :, k, :], w12[:, k, :].unsqueeze(2)
                                         .to_broadcast(wide), ALU.mult)
            link(last)
            dve.tensor_tensor(wd, ohr[:, :, 0, :], ohr[:, :, 1, :], ALU.add).then_inc(wd_done, 1)
            for k in range(2):
                step(0, k, total=UNITS)
            with dve.Fori(0, TURNS) as g:
                for k in range(2, 2 + RING):
                    step(g, k)
            for k in range(LOOP_END, BRANCH):
                step(0, k, total=UNITS)
            dve.wait_ge(xlist_done, 1)
            extra = dve.value_load(xlist[0:1, EXTRA:EXTRA + 1], min_val=0, max_val=EXTRA)
            with dve.If(extra < 1):
                for k in range(BRANCH, UNITS + 2):
                    step(0, k, total=UNITS)
            with dve.If(extra > 0):
                pair = dve.value_load(xlist[0:1, 0:1], min_val=0, max_val=UNITS - 1)
                for k in range(BRANCH, UNITS + 3):
                    step(0, k, total=UNITS + 1, pair=pair)
            with dve.If(extra > 1):
                with dve.Fori(1, extra) as j:
                    pair = dve.value_load(xlist[0:1, bass.ds(j, 1)], min_val=0, max_val=UNITS - 1)
                    u = j + UNITS
                    rows_in(u, 0)
                    add_bias(u, pair, 0, hb1, bank[3], ta_ps, a1_done)
                    add_bias(u, pair, 1, hb2, bank[4], tb_ps, a2_done)
                    bottle(u, pair)
                    results(u, 0, j * 16 + (1 + 16 * (UNITS // RING)))
            dve.wait_ge(wdt_ps, 1)
            dve.tensor_copy(prob[0:E, 1, 0:TILES * P], bank[7][0:E, :]).then_inc(wdt_done, 1)
            for t in range(TILES):
                dve.wait_ge(bl_ps, t + 1)
                dve.tensor_tensor(y0[:, t, :], bank[t][:, 0:D], h2[:, t, :], ALU.add).then_inc(y0_done, 1)
            dve.wait_ge(y0_done, TILES)
            for t in range(TILES):
                dve.wait_ge(s_pick[t], 16 * 2)
                for k in range(2):
                    last = dve.scalar_tensor_tensor(y0[:, t, :], picked[:, t, k, :], w12[:, k, t:t + 1], y0[:, t, :],
                                                    ALU.mult, ALU.add)
                    last.then_inc(out_done, 1) if k else link(last)

        @block.tensor
        def _(pe):
            mm, tr = nc.tensor.matmul, nc.tensor.transpose

            def channels_t(src, out_bank):
                tr(out_bank[:, 0:P], src[:, 0:D0], ident)
                return tr(out_bank[0:D1, P:2 * P], src[:, D0:D], ident)

            def embed(t):
                pe.wait_ge(s_xp[t], 16)
                if t >= 2:
                    pe.wait_ge(h_done, t - 1)
                for k in range(KT):
                    last = mm(bank[t % 2][:, 0:D], xp[:, t, k * P:(k + 1) * P], wt[:, k, :],
                              start=k == 0, stop=k == KT - 1)
                last.then_inc(embedded, 1)

            def xn_t(t):
                pe.wait_ge(xn_done, t + 1)
                if t >= 1:
                    pe.wait_ge(xnt_done, t)
                channels_t(xn[:, t % 2, :], bank[2]).then_inc(xnt_ps, 1)

            def qkv(t):
                if t >= 1:
                    pe.wait_ge(qkb_done, t)
                    pe.wait_ge(v_done, t)
                pe.wait_ge(xnt_done, t + 1)
                mm(bank[4][:, 0:2 * D], xnT[:, t % 2, 0, :], wqk0[:], start=True, stop=False)
                mm(bank[4][:, 0:2 * D], xnT[0:D1, t % 2, 1, :], wqk1[:], start=False, stop=True)\
                    .then_inc(qk_ps, 1)
                for i in range(2):
                    for half in range(2):
                        o = bank[5][64 * half:64 * half + 64, i * 96:(i + 1) * 96]
                        c = slice(96 * half, 96 * half + 96)
                        mm(o, xnT[:, t % 2, 0, i * 64:(i + 1) * 64], wv0[:, c], start=True, stop=False)
                        last = mm(o, xnT[0:D1, t % 2, 1, i * 64:(i + 1) * 64], wv1[:, c], start=False, stop=True)
                last.then_inc(v_ps, 1)

            def qk_t(t):
                pe.wait_ge(rot_done, t + 1)
                if t >= 1:
                    pe.wait_ge(kx1_done, t)
                    pe.wait_ge(kx0_done, t)
                r = rot[:, t % 2, :]
                channels_t(r[:, 0:D], bank[6])
                tr(bank[6][0:D1, 2 * P:3 * P], r[:, D + D0:2 * D], ident).then_inc(qt_ps, 1)
                tr(bank[7][:, 0:P], r[:, D:D + D0], ident).then_inc(kt_ps, 1)

            def scores(t):
                if t == 0:
                    pe.wait_ge(h_done, TILES)
                    pe.wait_ge(s_cast, 1)
                else:
                    pe.wait_ge(sub_done, t)
                causal = causb[:].rearrange("p n s -> p (n s)")
                mm(bank[0][:], identb[:], causal, start=True, stop=False, skip_group_check=True)
                mm(bank[1][:, 0:H1 * SEQ], identb[:], causal[:, 0:H1 * SEQ], start=True, stop=False,
                   skip_group_check=True)
                pe.wait_ge(kx1_done, t + 1)
                pe.wait_ge(kx0_done, t + 1)
                for i in range(2):
                    q = slice(64 * i, 64 * i + 64)
                    mm(bank[0][q, :], qT[:, t % 2, 0, q], kx0[:, t % 2, i, :], start=False, stop=True,
                       skip_group_check=True)
                for i in range(2):
                    q = slice(64 * i, 64 * i + 64)
                    last = mm(bank[1][q, 0:H1 * SEQ], qT[:, t % 2, 1, q], kx1[:, t % 2, i, :], start=False,
                              stop=True, skip_group_check=True)
                last.then_inc(sc_ps, 1)

            def p_t(t):
                pe.wait_ge(xnt_done, TILES) if t == 0 else pe.wait_ge(pt_done, t)
                pe.wait_ge(exp_done, t + 1)
                for c in range(HP):
                    last = tr(bank[2 + c // 4][:, (c % 4) * P:(c % 4 + 1) * P],
                              prob[:, t % 2, c * P:(c + 1) * P], ident)
                last.then_inc(pt_ps, 1)

            def values(t):
                if t == 0:
                    pe.wait_ge(qkb_done, TILES)
                else:
                    pe.wait_ge(att_done, t)
                pe.wait_ge(v_done, t + 1)
                pe.wait_ge(pt_done, t + 1)
                for c in range(HP):
                    for i in range(2):
                        q = slice(64 * i, 64 * i + 64)
                        last = mm(bank[4][q, c * VC:(c + 1) * VC],
                                  pT[:, t % 2, c * P + 64 * i:c * P + 64 * i + 64],
                                  vbd[:, t, i, c * VC:(c + 1) * VC], start=True, stop=True)
                last.then_inc(pv_ps, 1)

            def att_t(t):
                pe.wait_ge(kx1_done, TILES) if t == 0 else pe.wait_ge(at_done, t)
                pe.wait_ge(att_done, t + 1)
                channels_t(att[:, t % 2, :], bank[6]).then_inc(at_ps, 1)

            def project(t):
                if t == 0:
                    pe.wait_ge(sub_done, TILES)
                    pe.wait_ge(s_late, 16 * 7)
                else:
                    pe.wait_ge(st2, t)
                pe.wait_ge(at_done, t + 1)
                mm(bank[0][:, 0:D], attT[:, t % 2, 0, :], wo0[:], start=True, stop=False)
                mm(bank[0][:, 0:D], attT[0:D1, t % 2, 1, :], wo1[:], start=False, stop=True).then_inc(wo_ps, 1)

            def xn2_t(t):
                pe.wait_ge(pt_done, TILES) if t == 0 else pe.wait_ge(x2_done, t)
                pe.wait_ge(xn2_done, t + 1)
                channels_t(xn2[:, t, :], bank[2]).then_inc(x2_ps, 1)

            def gate(t):
                pe.wait_ge(v_done, TILES) if t == 0 else pe.wait_ge(lg_done, t)
                pe.wait_ge(x2_done, t + 1)
                o = bank[5][:, 0:E]
                mm(o, xn2T[:, t % 2, 0, :], g0[:], start=True, stop=False)
                mm(o, xn2T[0:D1, t % 2, 1, :], g1[:], start=False, stop=True).then_inc(lg_ps, 1)

            def rank(t):
                pe.wait_ge(kx0_done, TILES) if t == 0 else pe.wait_ge(rank_read, t)
                pe.wait_ge(oh_done, t + 1)
                o = bank[7][:, 0:E]
                for t2 in range(t + 1):
                    last = mm(o, trib[:] if t2 == t else onesb[:], ohb[:, t2, :], start=t2 == 0, stop=t2 == t)
                last.then_inc(rank_ps, 1)

            def keep_warm(products):
                for _ in range(products):
                    mm(bank[7][:, 0:D], blank[:, 0:P], blank[:], start=True, stop=True)

            pe.wait_ge(s_set, 1)
            keep_warm(WARM_1)
            pe.wait_ge(s_wt, 16)
            pe.wait_ge(s_cst, 16)
            pe.wait_ge(s_wqkv, 96)
            for stage, t in in_order([(embed, 0), (xn_t, AT_XNT), (qkv, AT_QKV), (qk_t, AT_QKT), (scores, AT_SCORES),
                                      (p_t, AT_PT), (values, AT_VALUES), (att_t, AT_ATT), (project, AT_PROJECT),
                                      (xn2_t, AT_X2T), (gate, AT_GATE), (rank, AT_RANK)]):
                stage(t)

            pe.wait_ge(att_done, TILES)
            for t in range(TILES):
                last = mm(bank[4][:, 0:E], onesb[:], ohb[:, t, :], start=t == 0,
                          stop=t == TILES - 1)
            last.then_inc(rank_ps, 1)
            def rows_t(u, s, arrived):
                pe.wait_ge(s_xs[s], arrived)
                pe.wait_ge(x_done, u)
                tr(bank[0][:, 0:P], xs[:, s, 0:D0], ident)
                tr(bank[0][:, P:2 * P], xs[:, s, D1:D], ident).then_inc(x_ps, 1)

            def w1(s, c):
                return ring[:, s, c * HID:(c + 1) * HID]

            def layer_1(u, s, b, arrived):
                pe.wait_ge(x_done, u + 1)
                pe.wait_ge(s_lo[s], arrived)
                mm(bank[1][0:64, :], xm[:, b, 64:P], w1(s, 0), start=True, stop=False, skip_group_check=True)
                mm(bank[1][64:P, :], xm[:, b, 0:64], w1(s, 1), start=True, stop=False, skip_group_check=True)
                mm(bank[1][:], xt[:, b, :], w1(s, 2), start=False, stop=True, skip_group_check=True)\
                    .then_inc(l1_ps, 1)

            def hidden_t(u, pre, out_bank, ready, done):
                pe.wait_ge(ready, u + 1)
                for k in range(HT):
                    last = tr(out_bank[:, k * P:(k + 1) * P], pre[:, k * P:(k + 1) * P], ident)
                last.then_inc(done, 1)

            def layer_2(u, s, arrived):
                pe.wait_ge(s_mid[s], arrived)
                pe.wait_ge(g1_done, u + 1)
                for k in range(HT):
                    for half in range(2):
                        q = slice(64 * half, 64 * half + 64)
                        c = MID + (half * HT + k) * HID
                        last = mm(bank[2][q, :], h1T[:, k, q], ring[:, s, c:c + HID], start=k == 0,
                                  stop=k == HT - 1)
                last.then_inc(l2_ps, 1)

            def layer_3(u, s, b, arrived):
                pe.wait_ge(s_hi[s], arrived)
                pe.wait_ge(g2_done, u + 1)
                for half in range(2):
                    q = slice(64 * half, 64 * half + 64)
                    for k in range(HT):
                        c = HI + (half * HT + k) * BOT
                        last = mm(bank[5][q, 0:CAP], ring[:, s, c:c + BOT], h2T[b][:, k, q], start=k == 0,
                                  stop=k == HT - 1)
                last.then_inc(l3_ps, 1)

            def layer_4(u, s):
                pe.wait_ge(z_done, u + 1)
                mm(bank[6][:, 0:D], zbd[:], ring[:, s, WC - D:WC], start=True, stop=True).then_inc(o_ps, 1)

            def step(g, k, total=None):
                def has(ahead):
                    return total is None or 0 <= k + ahead < total

                def at(ahead):
                    u, s, turn = unit_at(g, k + ahead)
                    return u, s, turn * 16 + 16

                if has(0):
                    layer_2(*at(0))
                if has(-2):
                    layer_4(*at(-2)[:2])
                if has(1):
                    hidden_t(at(1)[0], pre1, bank[3], c1_done, ta_ps)
                if has(2):
                    u, s, arrived = at(2)
                    layer_1(u, s, s % 2, arrived)
                if has(0):
                    hidden_t(at(0)[0], pre2, bank[4], c2_done, tb_ps)
                if has(3):
                    rows_t(*at(3))
                if has(-1):
                    u, s, arrived = at(-1)
                    layer_3(u, s, s % 2, arrived)

            pe.wait_ge(rank_read, TILES)
            keep_warm(WARM_2)
            rows_t(0, 0, 16)
            rows_t(1, 1, 16)
            layer_1(0, 0, 0, 16)
            rows_t(2, 2, 16)
            hidden_t(0, pre1, bank[3], c1_done, ta_ps)
            layer_1(1, 1, 1, 16)
            for k in range(2):
                step(0, k, UNITS)
            with pe.Fori(0, TURNS) as g:
                for k in range(2, 2 + RING):
                    step(g, k)
            for k in range(LOOP_END, BRANCH):
                step(0, k, UNITS)
            pe.wait_ge(xlist_done, 1)
            extra = pe.value_load(xlist[0:1, EXTRA:EXTRA + 1], min_val=0, max_val=EXTRA)
            with pe.If(extra < 1):
                for k in range(BRANCH, UNITS + 2):
                    step(0, k, UNITS)
            with pe.If(extra > 0):
                for k in range(BRANCH, UNITS + 3):
                    step(0, k, UNITS + 1)
            with pe.If(extra > 1):
                with pe.Fori(1, extra) as j:
                    u = j + UNITS
                    arrived = j * 16 + (UNITS // RING + 1) * 16
                    rows_t(u, 0, arrived)
                    layer_1(u, 0, 0, arrived)
                    hidden_t(u, pre1, bank[3], c1_done, ta_ps)
                    layer_2(u, 0, arrived)
                    hidden_t(u, pre2, bank[4], c2_done, tb_ps)
                    layer_3(u, 0, 0, arrived)
                    layer_4(u, 0)
            pe.wait_ge(wd_done, 1)
            for t in range(TILES):
                last = tr(bank[7][0:E, t * P:(t + 1) * P], wd[:, t, :], ident)
            last.then_inc(wdt_ps, 1)
            pe.wait_ge(wdt_done, 1)
            pe.wait_ge(a1_done, extra + UNITS)
            for t in range(TILES):
                mm(bank[t][:, 0:D], wdT[:, t, :], bl[:], start=True, stop=True).then_inc(bl_ps, 1)


def kernel(**inputs):
    import numpy as np
    import concourse.bacc as bacc
    from concourse.bass_utils import run_bass_kernel_spmd

    a = {k: np.asarray(v) for k, v in inputs.items()}
    x = a["x"].reshape(TILES, 2, 3, 8, 16, 8, 16).transpose(0, 4, 6, 2, 1, 3, 5)
    x = x.reshape(TILES, KT, P, P).transpose(0, 2, 1, 3).reshape(TILES, P, KT * P)
    wt = a["L0_tok_W"].T.reshape(KT, P, D).transpose(1, 0, 2)
    wqk = np.concatenate([a["L0_attn_Wq"].T, a["L0_attn_Wk"].T], 1)
    wv = a["L0_attn_Wv"].T.reshape(D, HP, 2, HD).transpose(0, 2, 1, 3).reshape(D, D)
    bv = a["L0_attn_bv"].reshape(HP, 2, HD).transpose(1, 0, 2).reshape(2, HP * HD)
    rows = np.concatenate([a["L0_tok_b"], a["L0_attn_bq"], a["L0_attn_bk"], a["L0_attn_bo"]])
    w1 = a["L0_ffn_W1"].reshape(UNITS, 2, D, HID)
    tails = np.concatenate([w1[:, 0, 0:D1], w1[:, 1, D0:D]], 1)
    w2 = a["L0_ffn_W2"].reshape(UNITS, 2, HT, P, HID).transpose(0, 3, 1, 2, 4).reshape(UNITS, P, W2C)
    w3 = a["L0_ffn_W3"].reshape(UNITS, 2, HT, P, BOT).transpose(0, 3, 1, 2, 4).reshape(UNITS, P, W3C)
    wl = a["L0_ffn_Wl"].reshape(UNITS, 2 * BOT, D)
    experts = np.concatenate([w1[:, 0, D1:D], w1[:, 1, 0:D0], tails, w2, w3, wl], 2)

    def by_hidden(b):
        return b.reshape(UNITS, 2, HT, P).transpose(3, 0, 2, 1).reshape(P, UNITS, HT * 2)
    b12 = np.stack([by_hidden(a["L0_ffn_b1"]), by_hidden(a["L0_ffn_b2"])], 2)
    b3 = a["L0_ffn_b3"].reshape(UNITS, 2 * BOT).T

    c = np.zeros((P, NC_), np.float32)

    def put(i, v):
        c[:, C_AT[i]:C_AT[i + 1]] = v
    p = np.arange(P)
    put(C_ID, p[:, None] == p[None, :])
    put(C_TRI, p[:, None] < p[None, :])
    put(C_CAUS, np.where(np.arange(SEQ)[None, :] > (p % SEQ)[:, None], -1e30, 0.0))
    inv = (1.0 / 10000.0 ** (np.arange(0, HD, 2, dtype=np.float32) / np.float32(HD))).astype(np.float32)
    ang = (p % SEQ).astype(np.float32)[:, None] * inv[None, :]
    cos, sin = np.cos(ang), np.sin(ang)
    scale = 1.0 / np.sqrt(np.float32(HD))
    cos2, sin2 = np.concatenate([cos, cos], 1), np.concatenate([-sin, sin], 1)
    put(C_COS, np.concatenate([cos2 * scale, cos2], 1))
    put(C_SIN, np.concatenate([sin2 * scale, sin2], 1))
    put(C_M0, (p // HD)[:, None] == np.arange(H0)[None, :])
    put(C_M1, (p // HD)[:, None] == np.arange(H1)[None, :])
    put(C_IOTA, np.arange(E)[None, :])
    put(C_PAIR, np.arange(UNITS)[None, :])

    arrays = {"xp": x, "wt": wt, "wqk": wqk, "wv": wv, "wo": a["L0_attn_Wo"].T, "gate": a["L0_ffn_gate_w"].T,
              "rows": rows, "bv": bv, "consts": c, "experts": experts, "b12": b12, "b3": b3,
              "bl": a["L0_ffn_bl"]}
    arrays = {f"in_{k}": np.ascontiguousarray(v) for k, v in arrays.items()}
    nc = bacc.Bacc("TRN2", target_bir_lowering=False, num_devices=1)
    args = [nc.dram_tensor(k, v.shape, F32, kind="ExternalInput").ap() for k, v in arrays.items()]
    out = nc.dram_tensor("out", (TOKENS, D), F32, kind="ExternalOutput").ap()
    vit_layer(nc, *args, out)
    r = run_bass_kernel_spmd(nc, [arrays], core_ids=[0])
    return r.results[0]["out"].reshape(TILES * 2, SEQ, D)
```

```python
from contextlib import ExitStack

import concourse.bass as bass
from concourse import mybir

F32 = mybir.dt.float32
BF16 = mybir.dt.bfloat16
I32 = mybir.dt.int32
U32 = mybir.dt.uint32
ALU = mybir.AluOpType
ACT = mybir.ActivationFunctionType
AX = mybir.AxisListType

P = 128
TOKENS, D = 512, 192
TILES = TOKENS // P
SEQ = 64
FEAT = 768
KT = FEAT // P
HEADS, HD = 12, 16
D0, D1 = 128, 64
H0, H1 = D0 // HD, D1 // HD
HP = HEADS // 2
VC = 2 * (HD + 1)
E, HID, BOT = 32, 512, 64
HT = HID // P
UNITS = E // 2
CAP = 64
EXTRA = 2 * TOKENS // CAP
STORED = UNITS - 3
NOWHERE = float(1 << 20)
RING = 4
W1C, W2C, W3C = 3 * HID, 2 * HT * HID, 2 * HT * BOT
MID = W1C
HI = W1C + W2C
WC = HI + W3C + D
EPS = 1e-5

WARM_1, WARM_2 = 6, 12
LAG = 3.0

C_ID, C_TRI, C_CAUS, C_COS, C_SIN, C_M0, C_M1, C_IOTA, C_PAIR = range(9)
C_COLS = [P, P, SEQ, 2 * HD, 2 * HD, H0, H1, P, UNITS]
C_AT = [sum(C_COLS[:i]) for i in range(len(C_COLS) + 1)]
NC_ = C_AT[-1]


def vit_layer(nc, xp_d, wt_d, proj_d, rows_d, consts_d, experts_d, biases_d, bl_d, out_d):
    slots_d = nc.dram_tensor("slots_d", ((UNITS + EXTRA) * P, D), F32, kind="Internal").ap()
    results_d = nc.dram_tensor("results_d", (STORED * P, D), F32, kind="Internal").ap()
    ctx = ExitStack()
    with ctx:
        def sb(name, shape, dt=F32):
            return ctx.enter_context(nc.sbuf_tensor(name, shape, dt))

        def sem(name):
            return ctx.enter_context(nc.semaphore(name))

        ring = sb("ring", [P, RING, WC])
        cst = sb("cst", [P, NC_])

        def const(i):
            return cst[:, C_AT[i]:C_AT[i + 1]]
        ident = const(C_ID)
        xp = sb("xp", [P, TILES, KT * P])
        wt = sb("wt", [P, KT, D])
        proj0, proj1 = sb("proj0", [P, 4 * D + E]), sb("proj1", [D1 + 1, 4 * D + E])
        wqk0, wv0, wo0, g0 = (proj0[:, a:b] for a, b in ((0, 2 * D), (2 * D, 3 * D), (3 * D, 4 * D), (4 * D, 4 * D + E)))
        wqk1, wv1, wo1, g1 = (proj1[:, a:b] for a, b in ((0, 2 * D), (2 * D, 3 * D), (3 * D, 4 * D), (4 * D, 4 * D + E)))
        rows = sb("rows", [P, D])
        biases = sb("biases", [P, UNITS * 4 * HT + UNITS])
        b12 = biases[:, 0:UNITS * 4 * HT].rearrange("p (u k n) -> p u k n", u=UNITS, k=2)
        b3 = biases[:, UNITS * 4 * HT:]
        bl = sb("bl", [E, D])
        identb = sb("identb", [P, P], BF16)
        causb = sb("causb", [P, H0, SEQ], BF16)
        trib = sb("trib", [P, P], BF16)
        onesb = sb("onesb", [P, P], BF16)
        halfneg = sb("halfneg", [P, 1])

        h = sb("h", [P, TILES, D])
        stats = sb("stats", [P, TILES, 6])
        mv = sb("mv", [P, TILES, 2])
        rstd = sb("rstd", [P, TILES])
        xn = sb("xn", [P, 2, D])
        xnT = sb("xnT", [P, 2, 2, P])
        qk_area = sb("qk_area", [P, 4, 2 * D])
        qkb, rcos = qk_area[:, 0:2], qk_area[:, 2:4]
        rsin = sb("rsin", [P, 2 * D])
        rot = sb("rot", [P, 2, 2 * D])
        qT = sb("qT", [P, 2, 2, P])
        kx0 = sb("kx0", [P, 2, 2, H0 * SEQ])
        kx1 = sb("kx1", [P, 2, 2, H1 * SEQ])
        vbd = sb("vbd", [P, TILES, 2, HP * VC])
        smax = sb("smax", [P, 2, HEADS])
        ssub = sb("ssub", [P, HEADS * SEQ])
        prob = sb("prob", [P, 2, HEADS * SEQ])
        pT = sb("pT", [P, 2, HP * P])
        rden = sb("rden", [P, 2, HEADS])
        att = sb("att", [P, 2, D])
        attT = sb("attT", [P, 2, 2, P])
        h2 = sb("h2", [P, TILES, D])
        xn2 = sb("xn2", [P, TILES, D])
        xn2T = sb("xn2T", [P, 2, 2, P])
        lg = sb("lg", [P, TILES, E])
        s4 = sb("s4", [P, 8, TILES])
        top = sb("top", [P, TILES, 8])
        topi = sb("topi", [P, TILES, 8], U32)
        oh = sb("oh", [P, TILES, 2, E])
        ohb = sb("ohb", [P, TILES, E], BF16)
        rtmp = kx0[:].rearrange("p a i n -> p (a i n)")
        ohr = rtmp[:, 0:TILES * 2 * E].rearrange("p (t k e) -> p t k e", t=TILES, k=2)
        gs, ge, prb, wd = (rtmp[:, i * P:(i + 1) * P].rearrange("p (t e) -> p t e", e=E) for i in range(2, 6))
        hot = [rtmp[:, i * 4 * P:(i + 1) * 4 * P].rearrange("p (t c) -> p t c", t=TILES) for i in (2, 3)]
        hotT = [pT[:].rearrange("p t c -> p (t c)")[:, i * 4 * P:(i + 1) * 4 * P] for i in range(3)]
        hotT.append(ssub[:, 0:4 * P])
        rank2 = sb("rank2", [P, TILES, 2])
        slot2 = sb("slot2", [P, 6, TILES, 2])
        rounds = sb("rounds", [P, TILES, 2], I32)
        first_sl = sb("first_sl", [P, TILES, 2], I32)
        spill_sl = sb("spill_sl", [P, TILES, 2], I32)
        sl = sb("sl", [P, TILES, 2], I32)
        w12 = sb("w12", [P, 2, TILES])
        cnti = sb("cnti", [P, E], I32)
        xtra = sb("xtra", [P, 6, UNITS])
        bext = sb("bext", [P, E])
        xcount = sb("xcount", [1, EXTRA])
        xlist = sb("xlist", [1, EXTRA + 1], I32)
        y0 = prob[:, 0, :].rearrange("p (t d) -> p t d", t=TILES)
        wdT = prob[0:E, 1, 0:TILES * P].rearrange("p (t n) -> p t n", t=TILES)
        xtab = prob[0:1, 1, TILES * P:TILES * P + EXTRA * UNITS].rearrange("p (j u) -> p j u", j=EXTRA)
        blank = sb("blank", [P, D])

        xs = kx1[:].rearrange("p a i n -> p (a i n)")[:, 0:RING * D].rearrange("p (s c) -> p s c", s=RING)
        after_wt = wt[:].rearrange("p k d -> p (k d)")
        xm = after_wt[:, 0:2 * P].rearrange("p (b s) -> p b s", b=2)
        ob = after_wt[:, 2 * P:2 * P + RING * D].rearrange("p (b d) -> p b d", b=RING)
        picked = qk_area[:].rearrange("p t (k d) -> p t k d", k=2)
        xt = sb("xt", [P, 2, P])
        pre1, pre2, hb1, hb2, h1T_, h2Ta = (
            xp[:].rearrange("p t k -> p (t k)")[:, i * HID:(i + 1) * HID] for i in range(6))
        h2Tb = sb("h2Tb", [P, HID])
        h2T_ = (h2Ta, h2Tb[:])
        h1T, *h2T = (v.rearrange("p (k s) -> p k s", k=HT) for v in (h1T_, *h2T_))
        zbd = sb("zbd", [P, P])
        scratch = sb("scratch", [1, 1])

        bank = [ctx.enter_context(nc.psum_tensor(f"bank{i}", [P, 512], F32)) for i in range(8)]

        s_xp = [sem(f"s_xp{t}") for t in range(TILES)]
        s_wt, s_cst, s_rows, s_proj, s_late = map(sem, ("s_wt", "s_cst", "s_rows", "s_proj", "s_late"))
        s_lo = [sem(f"s_lo{i}") for i in range(RING)]
        s_mid = [sem(f"s_mid{i}") for i in range(RING)]
        s_hi = [sem(f"s_hi{i}") for i in range(RING)]
        s_set = sem("s_set")
        s_cast = sem("s_cast")
        s_v = sem("s_v")
        s_blank, s_blank2, s_scat, s_spill, s_out = map(sem, ("s_blank", "s_blank2", "s_scat", "s_spill", "s_out"))
        s_xs = [sem(f"s_xs{i}") for i in range(RING)]
        (embedded, h_done, st1, rs1, xn_done, xnt_ps, xnt_done, qk_ps, v_ps, qkb_done, cos_done, v_done,
         rot_done, qt_ps, kt_ps, qt_done, kx1_done, kx0_done, sc_ps, sub_done, exp_done, pt_ps, pt_done,
         pv_ps, att_done, at_ps, at_done, wo_ps, st2, rs2, xn2_done, x2_ps, x2_done,
         lg_ps, lg_done, out_done) = (sem(n) for n in (
             "embedded h_done st1 rs1 xn_done xnt_ps xnt_done qk_ps v_ps qkb_done cos_done v_done "
             "rot_done qt_ps kt_ps qt_done kx1_done kx0_done sc_ps sub_done exp_done pt_ps pt_done "
             "pv_ps att_done at_ps at_done wo_ps st2 rs2 xn2_done x2_ps x2_done "
             "lg_ps lg_done out_done").split())
        gsub, gexp, oh_done, rank_ps, rank_read, first_done, xlist_done, wd_done, wdt_ps, wdt_done, bl_ps, y0_done = (
            sem(n) for n in ("gsub gexp oh_done rank_ps rank_read first_done xlist_done wd_done wdt_ps wdt_done "
                             "bl_ps y0_done").split())
        (x_ps, x_done, l1_ps, c1_done, ta_ps, a1_done, g1_done, l2_ps, c2_done, tb_ps, a2_done, g2_done,
         l3_ps, z_done, o_ps, o_done) = (sem(n) for n in (
             "x_ps x_done l1_ps c1_done ta_ps a1_done g1_done l2_ps c2_done tb_ps a2_done g2_done "
             "l3_ps z_done o_ps o_done").split())
        s_ob = [sem(f"s_ob{i}") for i in range(RING)]
        hot_done, hot_ps, hot_read, cmb_ps, cmb_done = (
            sem(n) for n in "hot_done hot_ps hot_read cmb_ps cmb_done".split())
        s_hot, s_picked = sem("s_hot"), sem("s_picked")
        s_pick = [sem(f"s_pick{t}") for t in range(TILES)]
        s_pool = sem("s_pool")

        block = ctx.enter_context(nc.Block())

        def in_order(stages):
            return [(fn, t) for _, t, fn in sorted(((t * LAG + at, t, fn) for fn, at in stages for t in range(TILES)),
                                                   key=lambda x: x[:2])]

        def unit_at(g, k):
            return g * RING + k, k % RING, g + k // RING

        TURNS = 2
        LOOP_END = 2 + TURNS * RING
        BRANCH = UNITS - 3

        @block.sync
        def _(sp):
            def load_lo(pair, s):
                sp.dma_start(ring[:, s, 0:MID], experts_d[pair, :, 0:MID]).then_inc(s_lo[s], 16)

            def load_mid(pair, s):
                sp.dma_start(ring[:, s, MID:HI], experts_d[pair, :, MID:HI]).then_inc(s_mid[s], 16)

            def load_hi(pair, s):
                sp.dma_start(ring[:, s, HI:WC], experts_d[pair, :, HI:WC]).then_inc(s_hi[s], 16)

            def load_rows(unit_, s):
                sp.dma_start(xs[:, s, :], by_unit[:, bass.ds(unit_, 1), :].rearrange("p u c -> p (u c)"))\
                    .then_inc(s_xs[s], 16)

            by_unit = slots_d.rearrange("(u p) c -> p u c", p=P)
            sp.dma_start(xp[:, 0, :], xp_d[0]).then_inc(s_xp[0], 16)
            sp.dma_start(wt[:], wt_d).then_inc(s_wt, 16)
            sp.dma_start(rows[:], rows_d.partition_broadcast(P)).then_inc(s_rows, 16)
            sp.dma_start(cst[:], consts_d).then_inc(s_cst, 16)
            sp.dma_start(xp[:, 1, :], xp_d[1]).then_inc(s_xp[1], 16)
            sp.dma_start(proj0[:], proj_d[0:D0]).then_inc(s_proj, 16)
            sp.dma_start(proj1[:], proj_d[D0:D + 1]).then_inc(s_proj, 16)
            for t in range(2, TILES):
                sp.dma_start(xp[:, t, :], xp_d[t]).then_inc(s_xp[t], 16)
            sp.dma_start(biases[:], biases_d).then_inc(s_late, 16)
            sp.dma_start(bl[:], bl_d).then_inc(s_late, 16)
            for u in range(RING):
                load_lo(u, u)
                load_mid(u, u)
                load_hi(u, u)
                if u == 1:
                    sp.wait_ge(s_set, 12)
                    zeros = blank[:].unsqueeze(1).to_broadcast([P, UNITS, D])
                    sp.dma_start(by_unit[:, 0:UNITS, :], zeros).then_inc(s_blank, 16)
            sp.dma_start(by_unit[:, UNITS:UNITS + EXTRA, :], zeros).then_inc(s_blank2, 16)
            sp.wait_ge(s_scat, 16 * 2 * TILES)
            for u in range(RING):
                load_rows(u, u)

            def store(unit_, s):
                sp.dma_start(results_d.rearrange("(u p) c -> p u c", p=P)[:, bass.ds(unit_, 1), :]
                             .rearrange("p u c -> p (u c)"), ob[:, s, :]).then_inc(s_ob[s], 16)

            def step(g, k, loads, pair=None):
                u = g * RING + k

                def has(ahead):
                    return loads is None or k + ahead < loads

                def whose(ahead):
                    return pair if pair is not None and k + ahead == UNITS else u + ahead
                if k >= 2:
                    sp.wait_ge(o_done, u - 1)
                    if loads is None or k - 2 < STORED:
                        store(u - 2, (k - 2) % RING)
                    if has(2):
                        load_hi(whose(2), (k + 2) % RING)
                if has(4):
                    if k < 2:
                        sp.wait_ge(l2_ps, u + 1)
                    load_mid(whose(4), k % RING)
                if has(6):
                    sp.wait_ge(l1_ps, u + 3)
                    load_rows(u + 6, (k + 2) % RING)
                    load_lo(whose(6), (k + 2) % RING)

            for u in (4, 5):
                sp.wait_ge(l1_ps, u - RING + 1)
                load_rows(u, u - RING)
                load_lo(u, u - RING)
            for k in range(2):
                step(0, k, UNITS)
            with sp.Fori(0, TURNS) as g:
                for k in range(2, 2 + RING):
                    step(g, k, None)
            sp.wait_ge(xlist_done, 1)
            extra = sp.value_load(xlist[0:1, EXTRA:EXTRA + 1], min_val=0, max_val=EXTRA)
            with sp.If(extra > 0):
                pair = sp.value_load(xlist[0:1, 0:1], min_val=0, max_val=UNITS - 1)
                sp.wait_ge(s_spill, 16 * 2 * TILES)
                for k in range(LOOP_END, UNITS):
                    step(0, k, UNITS + 1, pair)
            with sp.If(extra < 1):
                for k in range(LOOP_END, UNITS):
                    step(0, k, UNITS)
            with sp.If(extra > 1):
                with sp.Fori(1, extra) as j:
                    pair = sp.value_load(xlist[0:1, bass.ds(j, 1)], min_val=0, max_val=UNITS - 1)
                    sp.wait_ge(o_done, j + UNITS)
                    load_rows(j + UNITS, 0)
                    load_lo(pair, 0)
                    load_mid(pair, 0)
                    load_hi(pair, 0)
            for half in range(2):
                t = slice(2 * half, 2 * half + 2)
                sp.wait_ge(out_done, half + 1)
                sp.dma_start(out_d.rearrange("(t p) d -> p t d", p=P)[:, t, :], y0[:, t, :]).then_inc(s_out, 16)
            sp.wait_ge(s_out, 32)

        @block.gpsimd
        def _(pool):
            finished = []

            def done(ins, signal):
                ins.then_inc(signal, 1)
                finished.append(signal)
                pool.wait_ge(signal, finished.count(signal))

            done(pool.memset(blank[:], 0.0), s_set)
            done(pool.memset(halfneg[:], -0.5), s_set)
            done(pool.memset(vbd[:], 0.0), s_set)
            vr = vbd[:].rearrange("p t i (c v) -> p (t i c) v", v=VC)
            done(pool.memset(vr[0:64, :, HD:HD + 1], 1.0), s_set)
            done(pool.memset(vr[64:P, :, VC - 1:VC], 1.0), s_set)
            done(pool.memset(xnT[D1:D1 + 1, :, 1, :], 1.0), s_set)
            done(pool.memset(attT[D1:D1 + 1, :, 1, :], 1.0), s_set)
            done(pool.memset(qT[D1:P, :, 1, :], 0.0), s_set)
            done(pool.memset(kx1[D1:P], 0.0), s_set)
            done(pool.memset(onesb[:], 1.0), s_set)
            done(pool.memset(xt[:], 0.0), s_set)
            done(pool.memset(zbd[:], 0.0), s_set)
            for s in range(RING):
                done(pool.memset(scratch[:], 0.0), s_ob[s])

            def inverse_root(t, stat, ready):
                pool.wait_ge(stat, t + 1)
                done(pool.tensor_scalar(rstd[:, t:t + 1], mv[:, t, 1:2], EPS, None, ALU.add), s_pool)
                done(pool.tensor_tensor(rstd[:, t:t + 1], rstd[:, t:t + 1], halfneg[:], ALU.pow), ready)

            def ln1(t):
                inverse_root(t, st1, rs1)

            def rope_cos(t):
                if t == 0:
                    pool.wait_ge(s_cst, 16)
                pool.wait_ge(qkb_done, t + 1)
                if t >= 2:
                    pool.wait_ge(rot_done, t - 1)
                done(pool.tensor_tensor(rcos[:, t % 2, :].rearrange("p (a n d) -> p a n d", a=2, d=HD),
                                   qkb[:, t % 2, :].rearrange("p (a n d) -> p a n d", a=2, d=HD),
                                   const(C_COS).rearrange("p (a d) -> p a d", a=2).unsqueeze(2)
                                   .to_broadcast([P, 2, HEADS, HD]), ALU.mult), cos_done)

            def ln2(t):
                inverse_root(t, st2, rs2)

            def dispatch(t):
                pool.wait_ge(first_done, t + 1)
                pool.wait_ge(xn2_done, t + 1)
                if t == 0:
                    pool.wait_ge(s_blank, 16)
                for k in range(2):
                    pool.indirect_dma_start(slots_d, bass.IndirectOffsetOnAxis(ap=first_sl[:, t, k:k + 1], axis=0),
                                            xn2[:, t, :], None, bounds_check=UNITS * P - 1, oob_is_err=False)\
                        .then_inc(s_scat, 16)

            for stage, t in in_order([(ln1, 4.5), (rope_cos, 11), (ln2, 31.5),
                                      (dispatch, 42)]):
                stage(t)

            pool.wait_ge(s_blank2, 16)
            pool.wait_ge(xlist_done, 1)
            extra = pool.value_load(xlist[0:1, EXTRA:EXTRA + 1], min_val=0, max_val=EXTRA)
            with pool.If(extra > 0):
                for t in range(TILES):
                    for k in range(2):
                        pool.indirect_dma_start(slots_d, bass.IndirectOffsetOnAxis(ap=spill_sl[:, t, k:k + 1], axis=0),
                                                xn2[:, t, :], None, bounds_check=(UNITS + EXTRA) * P - 1,
                                                oob_is_err=False).then_inc(s_spill, 16)
            done(pool.memset(qk_area[:], 0.0), s_pool)
            for s in range(RING):
                pool.wait_ge(s_ob[s], 1 + 16 * len(range(s, STORED, RING)))
            for t in range(TILES):
                for k in range(2):
                    pool.indirect_dma_start(picked[:, t, k, :], None, results_d,
                                            bass.IndirectOffsetOnAxis(ap=sl[:, t, k:k + 1], axis=0),
                                            bounds_check=STORED * P - 1, oob_is_err=False).then_inc(s_pick[t], 16)

        @block.scalar
        def _(act):
            act.wait_ge(s_cst, 16)
            act.activation(identb[:], ident, ACT.Copy)
            act.activation(trib[:], const(C_TRI), ACT.Copy)
            act.activation(causb[:], const(C_CAUS).unsqueeze(1).to_broadcast([P, H0, SEQ]),
                           ACT.Copy).then_inc(s_cast, 1)
            act.wait_ge(s_set, 12)

            def copies(dst, src_bank, t, ready, done):
                act.wait_ge(ready, t + 1)
                act.activation(dst[:, t % 2, 0, :], src_bank[:, 0:P], ACT.Copy)
                act.activation(dst[0:D1, t % 2, 1, :], src_bank[0:D1, P:2 * P], ACT.Copy).then_inc(done, 1)

            def xn_t(t):
                if t >= 2:
                    act.wait_ge(v_ps, t - 1)
                copies(xnT, bank[2], t, xnt_ps, xnt_done)

            def qkv(t):
                act.wait_ge(qk_ps, t + 1)
                if t >= 2:
                    act.wait_ge(cos_done, t - 1)
                    act.wait_ge(rot_done, t - 1)
                act.activation(qkb[:, t % 2, :], bank[4][:, 0:2 * D], ACT.Copy).then_inc(qkb_done, 1)
                act.wait_ge(v_ps, t + 1)
                for half in range(2):
                    q = slice(64 * half, 64 * half + 64)
                    c = (HD + 1) * half
                    last = act.activation(
                        vbd[q, t].rearrange("p i (c v) -> p i c v", v=VC)[:, :, :, c:c + HD],
                        bank[5][q, 0:2 * HP * HD].rearrange("p (i c d) -> p i c d", i=2, d=HD), ACT.Copy)
                last.then_inc(v_done, 1)

            def q_t(t):
                if t >= 2:
                    act.wait_ge(sc_ps, t - 1)
                copies(qT, bank[6], t, qt_ps, qt_done)
                for n in range(H1):
                    last = act.activation(
                        kx1[0:D1, t % 2].rearrange("p i (n s) -> p i n s", s=SEQ)[:, :, n, :],
                        bank[6][0:D1, 2 * P:3 * P].rearrange("p (i s) -> p i s", s=SEQ),
                        ACT.Copy, scale=const(C_M1)[0:D1, n:n + 1])
                last.then_inc(kx1_done, 1)

            def exp_s(t):
                if t >= 2:
                    act.wait_ge(pt_ps, t - 1)
                act.wait_ge(sub_done, t + 1)
                act.activation(prob[:, t % 2, :], ssub[:], ACT.Exp).then_inc(exp_done, 1)

            def p_t(t):
                if t >= 2:
                    act.wait_ge(pv_ps, t - 1)
                act.wait_ge(pt_ps, t + 1)
                act.activation(pT[:, t % 2, 0:4 * P], bank[2][:], ACT.Copy)
                act.activation(pT[:, t % 2, 4 * P:6 * P], bank[3][:, 0:2 * P], ACT.Copy).then_inc(pt_done, 1)

            def att_t(t):
                if t >= 2:
                    act.wait_ge(wo_ps, t - 1)
                copies(attT, bank[6], t, at_ps, at_done)

            def xn2_t(t):
                if t >= 2:
                    act.wait_ge(lg_ps, t - 1)
                copies(xn2T, bank[2], t, x2_ps, x2_done)

            for stage, t in in_order([(xn_t, 5), (qkv, 10), (q_t, 14), (exp_s, 19.5), (p_t, 21.5),
                                      (att_t, 27.5), (xn2_t, 34.5)]):
                stage(t)

            def copy_1(u):
                act.wait_ge(l1_ps, u + 1)
                act.activation(pre1[:], bank[1][:], ACT.Copy).then_inc(c1_done, 1)

            def copy_2(u):
                act.wait_ge(l2_ps, u + 1)
                act.activation(pre2[:], bank[2][:], ACT.Copy).then_inc(c2_done, 1)

            def gelu_1(u):
                act.wait_ge(a1_done, u + 1)
                act.activation(h1T_, hb1[:], ACT.Gelu).then_inc(g1_done, 1)

            def gelu_2(u, b):
                act.wait_ge(a2_done, u + 1)
                act.activation(h2T_[b], hb2[:], ACT.Gelu).then_inc(g2_done, 1)

            def step(u, b, ahead=2):
                copy_2(u)
                if ahead >= 1:
                    gelu_1(u + 1)
                if ahead >= 2:
                    copy_1(u + 2)
                gelu_2(u, b)

            def turn_hot(n):
                act.wait_ge(hot_ps, n + 1)
                act.activation(hotT[n if isinstance(n, int) else 0], bank[7][:], ACT.Copy).then_inc(hot_read, 1)

            act.wait_ge(gsub, 1)
            act.activation(ge, gs, ACT.Exp).then_inc(gexp, 1)
            copy_1(0)
            gelu_1(0)
            copy_1(1)
            with act.Fori(0, LOOP_END // 2) as g:
                for b in range(2):
                    step(g * 2 + b, b)
            for k in range(LOOP_END, UNITS - 2):
                step(k, k % 2)
                if k < LOOP_END + 3:
                    turn_hot(k - LOOP_END)
            act.wait_ge(xlist_done, 1)
            extra = act.value_load(xlist[0:1, EXTRA:EXTRA + 1], min_val=0, max_val=EXTRA)
            with act.If(extra < 1):
                step(UNITS - 2, 0, 1)
                step(UNITS - 1, 1, 0)
            with act.If(extra > 0):
                turn_hot(3)
                step(UNITS - 2, 0, 2)
                step(UNITS - 1, 1, 1)
                step(UNITS, 0, 0)
            with act.If(extra > 1):
                with act.Fori(1, extra) as j:
                    copy_1(j + UNITS)
                    gelu_1(j + UNITS)
                    copy_2(j + UNITS)
                    gelu_2(j + UNITS, 0)
                    turn_hot(j + 3)

        @block.vector
        def _(dve):
            chain = [0]

            def link(ins):
                chain[0] += 1
                ins.then_inc(s_v, 1)
                dve.wait_ge(s_v, chain[0])

            def ln1_a(t):
                dve.wait_ge(embedded, t + 1)
                ins = dve.tensor_tensor(h[:, t, :], bank[t % 2][:, 0:D], rows[:], ALU.add)
                ins.then_inc(h_done, 1)
                dve.wait_ge(h_done, t + 1)
                link(dve.bn_stats(stats[:, t, :], h[:, t, :]))
                dve.bn_aggr(mv[:, t, :], stats[:, t, :]).then_inc(st1, 1)

            def ln1_b(t):
                dve.wait_ge(rs1, t + 1)
                if t >= 2:
                    dve.wait_ge(xnt_ps, t - 1)
                dve.wait_ge(st1, t + 1)
                dve.tensor_scalar(xn[:, t % 2, :], h[:, t, :], mv[:, t, 0:1], rstd[:, t:t + 1],
                                  ALU.subtract, ALU.mult).then_inc(xn_done, 1)

            def rope(t):
                if t == 0:
                    dve.wait_ge(s_cst, 16)
                    dve.wait_ge(s_set, 12)
                dve.wait_ge(qkb_done, t + 1)
                half_ = HD // 2
                src = qkb[:, t % 2, :].rearrange("p (a n d) -> p a n d", a=2, d=HD)
                dst = rsin[:].rearrange("p (a n d) -> p a n d", a=2, d=HD)
                sin = const(C_SIN).rearrange("p (a d) -> p a d", a=2).unsqueeze(2)\
                    .to_broadcast([P, 2, HEADS, HD])
                if t >= 1:
                    dve.wait_ge(rot_done, t)
                dve.tensor_tensor(dst[:, :, :, 0:half_], src[:, :, :, half_:HD], sin[:, :, :, 0:half_], ALU.mult)
                link(dve.tensor_tensor(dst[:, :, :, half_:HD], src[:, :, :, 0:half_], sin[:, :, :, half_:HD],
                                       ALU.mult))
                dve.wait_ge(cos_done, t + 1)
                if t >= 2:
                    dve.wait_ge(kt_ps, t - 1)
                dve.tensor_tensor(rot[:, t % 2, :], rcos[:, t % 2, :], rsin[:], ALU.add).then_inc(rot_done, 1)

            def keys(t):
                dve.wait_ge(kt_ps, t + 1)
                if t >= 2:
                    dve.wait_ge(sc_ps, t - 1)
                for i in range(2):
                    last = dve.tensor_tensor(
                        kx0[:, t % 2, i, :].rearrange("p (n s) -> p n s", s=SEQ),
                        bank[7][:, i * SEQ:(i + 1) * SEQ].unsqueeze(1).to_broadcast([P, H0, SEQ]),
                        const(C_M0).unsqueeze(2).to_broadcast([P, H0, SEQ]), ALU.mult)
                last.then_inc(kx0_done, 1)

            def scores(t):
                dve.wait_ge(sc_ps, t + 1)
                m = smax[:, t % 2, :]
                s0 = bank[0][:].rearrange("p (n s) -> p n s", s=SEQ)
                s1 = bank[1][:, 0:H1 * SEQ].rearrange("p (n s) -> p n s", s=SEQ)
                dve.tensor_reduce(m[:, 0:H0], s0, AX.X, ALU.max)
                link(dve.tensor_reduce(m[:, H0:HEADS], s1, AX.X, ALU.max))
                if t >= 1:
                    dve.wait_ge(exp_done, t)
                out = ssub[:].rearrange("p (n s) -> p n s", s=SEQ)
                dve.tensor_tensor(out[:, 0:H0, :], s0, m[:, 0:H0].unsqueeze(2).to_broadcast([P, H0, SEQ]), ALU.subtract)
                dve.tensor_tensor(out[:, H0:HEADS, :], s1, m[:, H0:HEADS].unsqueeze(2).to_broadcast([P, H1, SEQ]),
                                  ALU.subtract).then_inc(sub_done, 1)

            def attend(t):
                dve.wait_ge(pv_ps, t + 1)
                pv = bank[4][:, 0:HP * VC].rearrange("p (n v) -> p n v", v=HD + 1)
                if t >= 2:
                    dve.wait_ge(at_ps, t - 1)
                link(dve.reciprocal(rden[:, t % 2, :], pv[:, :, HD]))
                dve.tensor_tensor(att[:, t % 2, :].rearrange("p (n d) -> p n d", d=HD), pv[:, :, 0:HD],
                                  rden[:, t % 2, :].unsqueeze(2).to_broadcast([P, HEADS, HD]), ALU.mult)\
                    .then_inc(att_done, 1)

            def ln2_a(t):
                dve.wait_ge(wo_ps, t + 1)
                link(dve.tensor_tensor(h2[:, t, :], bank[0][:, 0:D], h[:, t, :], ALU.add))
                link(dve.bn_stats(stats[:, t, :], h2[:, t, :]))
                dve.bn_aggr(mv[:, t, :], stats[:, t, :]).then_inc(st2, 1)

            def ln2_b(t):
                dve.wait_ge(rs2, t + 1)
                dve.wait_ge(st2, t + 1)
                dve.tensor_scalar(xn2[:, t, :], h2[:, t, :], mv[:, t, 0:1], rstd[:, t:t + 1],
                                  ALU.subtract, ALU.mult).then_inc(xn2_done, 1)

            iota_p = const(C_IOTA)
            iota = iota_p[:, 0:E]

            def choose(t):
                dve.wait_ge(lg_ps, t + 1)
                dve.tensor_copy(lg[:, t, :], bank[5][:, 0:E]).then_inc(lg_done, 1)
                dve.wait_ge(lg_done, t + 1)
                link(dve.max(top[:, t, :], lg[:, t, :]))
                link(dve.max_index(topi[:, t, :], top[:, t, :], lg[:, t, :]))
                link(dve.tensor_tensor(oh[:, t], iota.unsqueeze(1).to_broadcast([P, 2, E]),
                                       topi[:, t, 0:2].unsqueeze(2).to_broadcast([P, 2, E]), ALU.is_equal))
                dve.tensor_tensor(ohb[:, t, :], oh[:, t, 0, :], oh[:, t, 1, :], ALU.add).then_inc(oh_done, 1)

            def place(t):
                dve.wait_ge(rank_ps, t + 1)
                if t == 0:
                    dve.wait_ge(sc_ps, TILES)
                dve.tensor_tensor(ohr[:, t], bank[7][:, 0:E].unsqueeze(1).to_broadcast([P, 2, E]),
                                  oh[:, t], ALU.mult).then_inc(rank_read, 1)
                dve.wait_ge(rank_read, t + 1)
                link(dve.tensor_reduce(rank2[:, t, :], ohr[:, t], AX.X, ALU.add))
                dve.tensor_scalar(slot2[:, 0, t, :], rank2[:, t, :], float(CAP), NOWHERE, ALU.is_ge, ALU.mult)
                link(dve.scalar_tensor_tensor(slot2[:, 1, t, :], topi[:, t, 0:2], float(CAP), rank2[:, t, :],
                                              ALU.mult, ALU.add))
                dve.tensor_tensor(first_sl[:, t, :], slot2[:, 0, t, :], slot2[:, 1, t, :], ALU.add)\
                    .then_inc(first_done, 1)

            dve.wait_ge(s_rows, 16)
            for stage, t in in_order([(ln1_a, 4.5), (ln1_b, 4.5), (rope, 11),
                                      (keys, 16), (scores, 19.5), (attend, 27), (ln2_a, 31.5),
                                      (ln2_b, 34), (choose, 39), (place, 42)]):
                stage(t)

            wide, both = [P, TILES, E], [P, TILES, 2, E]
            dve.tensor_tensor(gs, lg[:], top[:, :, 0:1].to_broadcast(wide), ALU.subtract).then_inc(gsub, 1)
            dve.wait_ge(rank_ps, TILES + 1)
            link(dve.tensor_scalar(cnti[:], bank[4][:, 0:E], float(CAP - 1), None, ALU.add))
            link(dve.tensor_scalar(cnti[:], cnti[:], 6, None, ALU.logical_shift_right))
            pairs = cnti[:].rearrange("p (u e) -> p u e", e=2)
            a, b, base, incl = (xtra[:, i, :] for i in range(4))
            link(dve.tensor_tensor(a, pairs[:, :, 0], pairs[:, :, 1], ALU.max))
            link(dve.tensor_scalar(a, a, 1.0, -1.0, ALU.max, ALU.add))
            src, dst, shift = a, b, 1
            while shift < UNITS:
                dve.tensor_copy(dst[:, 0:shift], src[:, 0:shift])
                link(dve.tensor_tensor(dst[:, shift:UNITS], src[:, shift:UNITS], src[:, 0:UNITS - shift], ALU.add))
                src, dst, shift = dst, (incl if dst is b else b), shift * 2
            incl_ = src
            link(dve.tensor_tensor(xtab, incl_[0:1, :].unsqueeze(1).to_broadcast([1, EXTRA, UNITS]),
                                   iota[0:1, 0:EXTRA].unsqueeze(2).to_broadcast([1, EXTRA, UNITS]), ALU.is_le))
            link(dve.tensor_reduce(xcount[:], xtab, AX.X, ALU.add))
            link(dve.tensor_scalar(xcount[:], xcount[:], float(UNITS - 1), None, ALU.min))
            dve.tensor_copy(xlist[:, 0:EXTRA], xcount[:])
            link(dve.tensor_copy(xlist[:, EXTRA:EXTRA + 1], incl_[0:1, UNITS - 1:UNITS]))
            base = xtra[:, 4, :]
            dve.memset(base[:, 0:1], 0.0)
            link(dve.tensor_copy(base[:, 1:UNITS], incl_[:, 0:UNITS - 1]))
            link(dve.tensor_tensor(base, base, const(C_PAIR), ALU.subtract))
            for e in range(2):
                last = dve.tensor_scalar(bext[:].rearrange("p (u e) -> p u e", e=2)[:, :, e], base,
                                         float(UNITS - 1), float(P), ALU.add, ALU.mult)
            link(last)
            beyond, plain, jump, round_, away = (slot2[:, i] for i in range(5))
            dve.tensor_copy(rounds[:], rank2[:])
            link(dve.tensor_tensor(ohr, bext[:].unsqueeze(1).unsqueeze(1).to_broadcast(both), oh[:], ALU.mult))
            dve.tensor_scalar(rounds[:], rounds[:], 6, 6, ALU.logical_shift_right, ALU.logical_shift_left)
            dve.tensor_scalar(beyond, rank2[:], float(CAP), None, ALU.is_ge)
            link(dve.tensor_reduce(jump, ohr, AX.X, ALU.add))
            link(dve.tensor_tensor(round_, rounds[:], jump, ALU.add))
            dve.tensor_scalar(away, beyond, -NOWHERE, NOWHERE, ALU.mult, ALU.add)
            link(dve.tensor_tensor(round_, round_, beyond, ALU.mult))
            link(dve.tensor_tensor(plain, plain, round_, ALU.add))
            dve.tensor_copy(sl[:], plain)
            dve.tensor_tensor(spill_sl[:], plain, away, ALU.add).then_inc(xlist_done, 1)
            def rows_in(u, b):
                dve.wait_ge(x_ps, u + 1)
                dve.tensor_copy(xm[:, b, :], bank[0][:, 64:64 + P])
                dve.tensor_copy(xt[0:64, b, 0:64], bank[0][0:64, 0:64])
                dve.tensor_copy(xt[64:P, b, 64:P], bank[0][64:P, P + 64:2 * P]).then_inc(x_done, 1)

            def add_bias(u, pair, k, out, bank_, ready, done):
                dve.wait_ge(ready, u + 1)
                dve.tensor_tensor(out[:].rearrange("p (k s) -> p k s", s=CAP),
                                  bank_[:].rearrange("p (k s) -> p k s", s=CAP),
                                  pair_bias(pair, k).to_broadcast([P, 2 * HT, CAP]), ALU.add).then_inc(done, 1)

            def pair_bias(pair, k):
                return b12[:, bass.ds(pair, 1), k, :].rearrange("p u k -> p (u k)").unsqueeze(2)

            def bottle(u, pair):
                dve.wait_ge(l3_ps, u + 1)
                for half in range(2):
                    q = slice(64 * half, 64 * half + 64)
                    last = dve.tensor_scalar(zbd[q, q], bank[5][q, 0:CAP], b3[q, bass.ds(pair, 1)], None, ALU.add)
                last.then_inc(z_done, 1)

            def results(u, s, sent):
                dve.wait_ge(o_ps, u + 1)
                dve.wait_ge(s_ob[s], sent)
                dve.tensor_copy(ob[:, s, :], bank[6][:, 0:D]).then_inc(o_done, 1)

            def step(g, k, first=0, total=None, pair=None):
                def has(ahead):
                    return total is None or first <= k + ahead < total

                def whose(ahead):
                    return pair if k + ahead == UNITS and pair is not None else g * RING + k + ahead
                u = g * RING + k
                if has(-2):
                    _, s, turn = unit_at(g, k - 2)
                    results(u - 2, s, turn * 16 + 1)
                if has(1):
                    add_bias(u + 1, whose(1), 0, hb1, bank[3], ta_ps, a1_done)
                if has(0):
                    add_bias(u, whose(0), 1, hb2, bank[4], tb_ps, a2_done)
                if has(3):
                    rows_in(u + 3, (k + 3) % 2)
                if has(-1):
                    bottle(u - 1, whose(-1))

            dve.wait_ge(s_late, 32)
            rows_in(0, 0)
            rows_in(1, 1)
            add_bias(0, 0, 0, hb1, bank[3], ta_ps, a1_done)
            rows_in(2, 0)
            z, rz, den = (s4[:, i, :] for i in range(3))
            dve.wait_ge(gexp, 1)
            link(dve.tensor_reduce(z, ge, AX.X, ALU.add))
            link(dve.reciprocal(rz, z))
            link(dve.tensor_tensor(prb, ge, rz.unsqueeze(2).to_broadcast(wide), ALU.mult))
            link(dve.tensor_tensor(ohr, prb.unsqueeze(2).to_broadcast(both), oh[:], ALU.mult))
            for k in range(2):
                last = dve.tensor_reduce(w12[:, k, :], ohr[:, :, k, :], AX.X, ALU.add)
            link(last)
            link(dve.tensor_tensor(den, w12[:, 0, :], w12[:, 1, :], ALU.add))
            link(dve.tensor_scalar(den, den, 1e-20, None, ALU.add))
            link(dve.reciprocal(rz, den))
            link(dve.tensor_tensor(w12[:], w12[:], rz.unsqueeze(1).to_broadcast([P, 2, TILES]), ALU.mult))
            rel = slot2[:, 5]
            dve.tensor_scalar(rel, plain, -float(STORED * P), None, ALU.add)

            def one_hot(n, before):
                if not (isinstance(n, int) and n == 0):
                    dve.wait_ge(hot_ps, n)
                    link2(dve.tensor_scalar(rel, rel, -float(P), None, ALU.add), before)
                for k in range(2):
                    for t in range(TILES):
                        last = dve.tensor_scalar(hot[k][:, t, :], iota_p, rel[:, t, k:k + 1], w12[:, k, t:t + 1],
                                                 ALU.is_equal, ALU.mult)
                link2(last, before + 1)
                dve.tensor_tensor(hot[0], hot[0], hot[1], ALU.add).then_inc(hot_done, 1)

            def link2(ins, before):
                ins.then_inc(s_hot, 1)
                dve.wait_ge(s_hot, before + 1)

            for k in range(2):
                last = dve.tensor_tensor(ohr[:, :, k, :], oh[:, :, k, :], w12[:, k, :].unsqueeze(2)
                                         .to_broadcast(wide), ALU.mult)
            link(last)
            dve.tensor_tensor(wd, ohr[:, :, 0, :], ohr[:, :, 1, :], ALU.add).then_inc(wd_done, 1)

            def base_rows(half):
                dve.wait_ge(bl_ps, half + 1)
                for t in range(2 * half, 2 * half + 2):
                    last = dve.tensor_tensor(y0[:, t, :], bank[7][:, (t % 2) * D:(t % 2 + 1) * D], h2[:, t, :], ALU.add)
                last.then_inc(y0_done, 1)

            def add_combined(so_far, signal):
                for half in range(2):
                    dve.wait_ge(cmb_ps, so_far * 2 + (half - 1))
                    y = y0[:, 2 * half:2 * half + 2, :].rearrange("p t d -> p (t d)")
                    dve.tensor_tensor(y, y, bank[half][:, 0:2 * D], ALU.add).then_inc(signal, 1)

            def add_picked(t):
                dve.wait_ge(s_pick[t], 16 * 2)
                for k in range(2):
                    last = dve.scalar_tensor_tensor(y0[:, t, :], picked[:, t, k, :], w12[:, k, t:t + 1], y0[:, t, :],
                                                    ALU.mult, ALU.add).then_inc(s_picked, 1)
                    dve.wait_ge(s_picked, 2 * t + k + 1)

            def aside(k):
                if k == 14:
                    dve.wait_ge(wdt_ps, 1)
                    dve.tensor_copy(prob[0:E, 1, 0:TILES * P], bank[7][0:E, :]).then_inc(wdt_done, 1)
                if k == 15:
                    base_rows(0)
                if k == 16:
                    base_rows(1)
                    dve.wait_ge(y0_done, 2)
                if k == 17:
                    add_picked(0)
                    add_picked(1)
            for k in range(2):
                step(0, k, total=UNITS)
            with dve.Fori(0, TURNS) as g:
                for k in range(2, 2 + RING):
                    step(g, k)
            for k in range(LOOP_END, BRANCH):
                one_hot(k - LOOP_END, 2 * (k - LOOP_END) - 1 if k > LOOP_END else -1)
                step(0, k, total=UNITS)
            dve.wait_ge(xlist_done, 1)
            extra = dve.value_load(xlist[0:1, EXTRA:EXTRA + 1], min_val=0, max_val=EXTRA)
            with dve.If(extra < 1):
                for k in range(BRANCH, UNITS + 2):
                    step(0, k, total=UNITS)
                    aside(k)
            with dve.If(extra > 0):
                pair = dve.value_load(xlist[0:1, 0:1], min_val=0, max_val=UNITS - 1)
                one_hot(3, 5)
                for k in range(BRANCH, UNITS + 3):
                    step(0, k, total=UNITS + 1, pair=pair)
                    aside(k)
            with dve.If(extra > 1):
                with dve.Fori(1, extra) as j:
                    pair = dve.value_load(xlist[0:1, bass.ds(j, 1)], min_val=0, max_val=UNITS - 1)
                    u = j + UNITS
                    add_combined(j + 3, cmb_done)
                    dve.wait_ge(cmb_done, j * 2)
                    rows_in(u, 0)
                    add_bias(u, pair, 0, hb1, bank[3], ta_ps, a1_done)
                    add_bias(u, pair, 1, hb2, bank[4], tb_ps, a2_done)
                    bottle(u, pair)
                    results(u, 0, 1 + 16 * (UNITS // RING))
                    one_hot(j + 3, j * 2 + 5)
            for t in range(2, TILES):
                add_picked(t)
            add_combined(extra + 3, out_done)

        @block.tensor
        def _(pe):
            mm, tr = nc.tensor.matmul, nc.tensor.transpose

            def channels_t(src, out_bank):
                tr(out_bank[:, 0:P], src[:, 0:D0], ident)
                return tr(out_bank[0:D1, P:2 * P], src[:, D0:D], ident)

            def embed(t):
                pe.wait_ge(s_xp[t], 16)
                if t >= 2:
                    pe.wait_ge(h_done, t - 1)
                for k in range(KT):
                    last = mm(bank[t % 2][:, 0:D], xp[:, t, k * P:(k + 1) * P], wt[:, k, :],
                              start=k == 0, stop=k == KT - 1)
                last.then_inc(embedded, 1)

            def xn_t(t):
                if t == 0:
                    pe.wait_ge(s_cst, 16)
                pe.wait_ge(xn_done, t + 1)
                if t >= 1:
                    pe.wait_ge(xnt_done, t)
                channels_t(xn[:, t % 2, :], bank[2]).then_inc(xnt_ps, 1)

            def qkv(t):
                if t == 0:
                    pe.wait_ge(s_proj, 32)
                if t >= 1:
                    pe.wait_ge(qkb_done, t)
                    pe.wait_ge(v_done, t)
                pe.wait_ge(xnt_done, t + 1)
                mm(bank[4][:, 0:2 * D], xnT[:, t % 2, 0, :], wqk0, start=True, stop=False)
                mm(bank[4][:, 0:2 * D], xnT[0:D1 + 1, t % 2, 1, :], wqk1, start=False, stop=True)\
                    .then_inc(qk_ps, 1)
                for i in range(2):
                    for half in range(2):
                        o = bank[5][64 * half:64 * half + 64, i * 96:(i + 1) * 96]
                        c = slice(96 * half, 96 * half + 96)
                        mm(o, xnT[:, t % 2, 0, i * 64:(i + 1) * 64], wv0[:, c], start=True, stop=False)
                        last = mm(o, xnT[0:D1 + 1, t % 2, 1, i * 64:(i + 1) * 64], wv1[:, c], start=False, stop=True)
                last.then_inc(v_ps, 1)

            def qk_t(t):
                pe.wait_ge(rot_done, t + 1)
                if t >= 1:
                    pe.wait_ge(kx1_done, t)
                    pe.wait_ge(kx0_done, t)
                r = rot[:, t % 2, :]
                channels_t(r[:, 0:D], bank[6])
                tr(bank[6][0:D1, 2 * P:3 * P], r[:, D + D0:2 * D], ident).then_inc(qt_ps, 1)
                tr(bank[7][:, 0:P], r[:, D:D + D0], ident).then_inc(kt_ps, 1)

            def scores(t):
                if t == 0:
                    pe.wait_ge(h_done, TILES)
                    pe.wait_ge(s_cast, 1)
                else:
                    pe.wait_ge(sub_done, t)
                causal = causb[:].rearrange("p n s -> p (n s)")
                mm(bank[0][:], identb[:], causal, start=True, stop=False, skip_group_check=True)
                mm(bank[1][:, 0:H1 * SEQ], identb[:], causal[:, 0:H1 * SEQ], start=True, stop=False,
                   skip_group_check=True)
                pe.wait_ge(kx1_done, t + 1)
                pe.wait_ge(kx0_done, t + 1)
                for i in range(2):
                    q = slice(64 * i, 64 * i + 64)
                    mm(bank[0][q, :], qT[:, t % 2, 0, q], kx0[:, t % 2, i, :], start=False, stop=True,
                       skip_group_check=True)
                for i in range(2):
                    q = slice(64 * i, 64 * i + 64)
                    last = mm(bank[1][q, 0:H1 * SEQ], qT[:, t % 2, 1, q], kx1[:, t % 2, i, :], start=False,
                              stop=True, skip_group_check=True)
                last.then_inc(sc_ps, 1)

            def p_t(t):
                pe.wait_ge(xnt_done, TILES) if t == 0 else pe.wait_ge(pt_done, t)
                pe.wait_ge(exp_done, t + 1)
                for c in range(HP):
                    last = tr(bank[2 + c // 4][:, (c % 4) * P:(c % 4 + 1) * P],
                              prob[:, t % 2, c * P:(c + 1) * P], ident)
                last.then_inc(pt_ps, 1)

            def values(t):
                if t == 0:
                    pe.wait_ge(qkb_done, TILES)
                else:
                    pe.wait_ge(att_done, t)
                pe.wait_ge(v_done, t + 1)
                pe.wait_ge(pt_done, t + 1)
                for c in range(HP):
                    for i in range(2):
                        q = slice(64 * i, 64 * i + 64)
                        last = mm(bank[4][q, c * VC:(c + 1) * VC],
                                  pT[:, t % 2, c * P + 64 * i:c * P + 64 * i + 64],
                                  vbd[:, t, i, c * VC:(c + 1) * VC], start=True, stop=True)
                last.then_inc(pv_ps, 1)

            def att_t(t):
                pe.wait_ge(kx1_done, TILES) if t == 0 else pe.wait_ge(at_done, t)
                pe.wait_ge(att_done, t + 1)
                channels_t(att[:, t % 2, :], bank[6]).then_inc(at_ps, 1)

            def project(t):
                if t == 0:
                    pe.wait_ge(sub_done, TILES)
                else:
                    pe.wait_ge(st2, t)
                pe.wait_ge(at_done, t + 1)
                mm(bank[0][:, 0:D], attT[:, t % 2, 0, :], wo0, start=True, stop=False)
                mm(bank[0][:, 0:D], attT[0:D1 + 1, t % 2, 1, :], wo1, start=False, stop=True).then_inc(wo_ps, 1)

            def xn2_t(t):
                pe.wait_ge(pt_done, TILES) if t == 0 else pe.wait_ge(x2_done, t)
                pe.wait_ge(xn2_done, t + 1)
                channels_t(xn2[:, t, :], bank[2]).then_inc(x2_ps, 1)

            def gate(t):
                pe.wait_ge(v_done, TILES) if t == 0 else pe.wait_ge(lg_done, t)
                pe.wait_ge(x2_done, t + 1)
                o = bank[5][:, 0:E]
                mm(o, xn2T[:, t % 2, 0, :], g0, start=True, stop=False)
                mm(o, xn2T[0:D1, t % 2, 1, :], g1[0:D1], start=False, stop=True).then_inc(lg_ps, 1)

            def rank(t):
                pe.wait_ge(kx0_done, TILES) if t == 0 else pe.wait_ge(rank_read, t)
                pe.wait_ge(oh_done, t + 1)
                o = bank[7][:, 0:E]
                for t2 in range(t + 1):
                    last = mm(o, trib[:] if t2 == t else onesb[:], ohb[:, t2, :], start=t2 == 0, stop=t2 == t)
                last.then_inc(rank_ps, 1)

            def keep_warm(products):
                for _ in range(products):
                    mm(bank[7][:, 0:D], blank[:, 0:P], blank[:], start=True, stop=True)

            pe.wait_ge(s_set, 1)
            keep_warm(WARM_1)
            pe.wait_ge(s_wt, 16)
            for stage, t in in_order([(embed, 0), (xn_t, 5), (qkv, 8.5), (qk_t, 14), (scores, 17.5),
                                      (p_t, 21.5), (values, 25), (att_t, 27.5), (project, 30.5),
                                      (xn2_t, 34.5), (gate, 37.5), (rank, 40.5)]):
                stage(t)

            pe.wait_ge(att_done, TILES)
            for t in range(TILES):
                last = mm(bank[4][:, 0:E], onesb[:], ohb[:, t, :], start=t == 0,
                          stop=t == TILES - 1)
            last.then_inc(rank_ps, 1)
            def rows_t(u, s, arrived):
                pe.wait_ge(s_xs[s], arrived)
                pe.wait_ge(x_done, u)
                tr(bank[0][:, 0:P], xs[:, s, 0:D0], ident)
                tr(bank[0][:, P:2 * P], xs[:, s, D1:D], ident).then_inc(x_ps, 1)

            def w1(s, c):
                return ring[:, s, c * HID:(c + 1) * HID]

            def layer_1(u, s, b, arrived):
                pe.wait_ge(x_done, u + 1)
                pe.wait_ge(s_lo[s], arrived)
                mm(bank[1][0:64, :], xm[:, b, 64:P], w1(s, 0), start=True, stop=False, skip_group_check=True)
                mm(bank[1][64:P, :], xm[:, b, 0:64], w1(s, 1), start=True, stop=False, skip_group_check=True)
                mm(bank[1][:], xt[:, b, :], w1(s, 2), start=False, stop=True, skip_group_check=True)\
                    .then_inc(l1_ps, 1)

            def hidden_t(u, pre, out_bank, ready, done):
                pe.wait_ge(ready, u + 1)
                for k in range(HT):
                    last = tr(out_bank[:, k * P:(k + 1) * P], pre[:, k * P:(k + 1) * P], ident)
                last.then_inc(done, 1)

            def layer_2(u, s, arrived):
                pe.wait_ge(s_mid[s], arrived)
                pe.wait_ge(g1_done, u + 1)
                for k in range(HT):
                    for half in range(2):
                        q = slice(64 * half, 64 * half + 64)
                        c = MID + (half * HT + k) * HID
                        last = mm(bank[2][q, :], h1T[:, k, q], ring[:, s, c:c + HID], start=k == 0,
                                  stop=k == HT - 1)
                last.then_inc(l2_ps, 1)

            def layer_3(u, s, b, arrived):
                pe.wait_ge(s_hi[s], arrived)
                pe.wait_ge(g2_done, u + 1)
                for half in range(2):
                    q = slice(64 * half, 64 * half + 64)
                    for k in range(HT):
                        c = HI + (half * HT + k) * BOT
                        last = mm(bank[5][q, 0:CAP], ring[:, s, c:c + BOT], h2T[b][:, k, q], start=k == 0,
                                  stop=k == HT - 1)
                last.then_inc(l3_ps, 1)

            def layer_4(u, s):
                pe.wait_ge(z_done, u + 1)
                mm(bank[6][:, 0:D], zbd[:], ring[:, s, WC - D:WC], start=True, stop=True).then_inc(o_ps, 1)

            def step(g, k, total=None):
                def has(ahead):
                    return total is None or 0 <= k + ahead < total

                def at(ahead):
                    u, s, turn = unit_at(g, k + ahead)
                    return u, s, turn * 16 + 16

                if has(0):
                    layer_2(*at(0))
                if has(-2):
                    layer_4(*at(-2)[:2])
                if has(1):
                    hidden_t(at(1)[0], pre1, bank[3], c1_done, ta_ps)
                if has(2):
                    u, s, arrived = at(2)
                    layer_1(u, s, s % 2, arrived)
                if has(0):
                    hidden_t(at(0)[0], pre2, bank[4], c2_done, tb_ps)
                if has(3):
                    rows_t(*at(3))
                if has(-1):
                    u, s, arrived = at(-1)
                    layer_3(u, s, s % 2, arrived)

            def turn_hot(n):
                pe.wait_ge(hot_done, n + 1)
                if not (isinstance(n, int) and n == 0):
                    pe.wait_ge(hot_read, n)
                for t in range(TILES):
                    last = tr(bank[7][:, t * P:(t + 1) * P], hot[0][:, t, :], ident)
                last.then_inc(hot_ps, 1)

            def combine(n):
                pe.wait_ge(o_done, n + (STORED + 1))
                pe.wait_ge(hot_read, n + 1)
                if isinstance(n, int) and n == 0:
                    pe.wait_ge(x_done, UNITS)
                    pe.wait_ge(c1_done, UNITS)
                for t in range(TILES):
                    last = mm(bank[t // 2][:, (t % 2) * D:(t % 2 + 1) * D],
                              hotT[n if isinstance(n, int) else 0][:, t * P:(t + 1) * P],
                              ob[:, (n + STORED) % RING if isinstance(n, int) else 0, :],
                              start=(not isinstance(n, int) or n == 0) and t % 2 == 0, stop=True,
                              skip_group_check=True)
                    if t % 2 == 1:
                        last.then_inc(cmb_ps, 1)

            def aside(k, turned):
                if k == 14:
                    pe.wait_ge(s_late, 32)
                    pe.wait_ge(hot_read, turned)
                    for t in range(TILES):
                        last = tr(bank[7][0:E, t * P:(t + 1) * P], wd[:, t, :], ident)
                    last.then_inc(wdt_ps, 1)
                if k in (15, 16):
                    pe.wait_ge(wdt_done, 1) if k == 15 else pe.wait_ge(y0_done, 1)
                    for t in range(2 * (k - 15), 2 * (k - 15) + 2):
                        last = mm(bank[7][:, (t % 2) * D:(t % 2 + 1) * D], wdT[:, t, :], bl[:], start=True, stop=True)
                    last.then_inc(bl_ps, 1)
                if k in (16, 17):
                    combine(k - 16)

            pe.wait_ge(rank_read, TILES)
            keep_warm(WARM_2)
            rows_t(0, 0, 16)
            layer_1(0, 0, 0, 16)
            rows_t(1, 1, 16)
            hidden_t(0, pre1, bank[3], c1_done, ta_ps)
            layer_1(1, 1, 1, 16)
            rows_t(2, 2, 16)
            for k in range(2):
                step(0, k, UNITS)
            with pe.Fori(0, TURNS) as g:
                for k in range(2, 2 + RING):
                    step(g, k)
            for k in range(LOOP_END, BRANCH):
                step(0, k, UNITS)
                turn_hot(k - LOOP_END)
            pe.wait_ge(xlist_done, 1)
            extra = pe.value_load(xlist[0:1, EXTRA:EXTRA + 1], min_val=0, max_val=EXTRA)
            with pe.If(extra < 1):
                for k in range(BRANCH, UNITS + 2):
                    step(0, k, UNITS)
                    aside(k, 3)
                combine(2)
            with pe.If(extra > 0):
                for k in range(BRANCH, UNITS + 3):
                    step(0, k, UNITS + 1)
                    if k == BRANCH:
                        turn_hot(3)
                    aside(k, 4)
                combine(2)
                combine(3)
            with pe.If(extra > 1):
                with pe.Fori(1, extra) as j:
                    u = j + UNITS
                    arrived = j * 16 + (UNITS // RING + 1) * 16
                    pe.wait_ge(cmb_done, j * 2)
                    rows_t(u, 0, arrived)
                    layer_1(u, 0, 0, arrived)
                    hidden_t(u, pre1, bank[3], c1_done, ta_ps)
                    layer_2(u, 0, arrived)
                    hidden_t(u, pre2, bank[4], c2_done, tb_ps)
                    layer_3(u, 0, 0, arrived)
                    layer_4(u, 0)
                    turn_hot(j + 3)
                    combine(j + 3)


def kernel(**inputs):
    import numpy as np
    import concourse.bacc as bacc
    from concourse.bass_utils import run_bass_kernel_spmd

    a = {k: np.asarray(v) for k, v in inputs.items()}
    x = a["x"].reshape(TILES, 2, 3, 8, 16, 8, 16).transpose(0, 4, 6, 2, 1, 3, 5)
    x = x.reshape(TILES, KT, P, P).transpose(0, 2, 1, 3).reshape(TILES, P, KT * P)
    wt = a["L0_tok_W"].T.reshape(KT, P, D).transpose(1, 0, 2)
    wv = a["L0_attn_Wv"].T.reshape(D, HP, 2, HD).transpose(0, 2, 1, 3).reshape(D, D)
    bv = a["L0_attn_bv"].reshape(HP, 2, HD).transpose(1, 0, 2).reshape(D)
    proj = np.concatenate([a["L0_attn_Wq"].T, a["L0_attn_Wk"].T, wv, a["L0_attn_Wo"].T, a["L0_ffn_gate_w"].T], 1)
    row = np.concatenate([a["L0_attn_bq"], a["L0_attn_bk"], bv, a["L0_attn_bo"], np.zeros(E, np.float32)])
    proj = np.concatenate([proj, row[None]], 0)
    w1 = a["L0_ffn_W1"].reshape(UNITS, 2, D, HID)
    tails = np.concatenate([w1[:, 0, 0:D1], w1[:, 1, D0:D]], 1)
    w2 = a["L0_ffn_W2"].reshape(UNITS, 2, HT, P, HID).transpose(0, 3, 1, 2, 4).reshape(UNITS, P, W2C)
    w3 = a["L0_ffn_W3"].reshape(UNITS, 2, HT, P, BOT).transpose(0, 3, 1, 2, 4).reshape(UNITS, P, W3C)
    wl = a["L0_ffn_Wl"].reshape(UNITS, 2 * BOT, D)
    experts = np.concatenate([w1[:, 0, D1:D], w1[:, 1, 0:D0], tails, w2, w3, wl], 2)

    def by_hidden(b):
        return b.reshape(UNITS, 2, HT, P).transpose(3, 0, 2, 1).reshape(P, UNITS, HT * 2)
    b12 = np.stack([by_hidden(a["L0_ffn_b1"]), by_hidden(a["L0_ffn_b2"])], 2)
    b3 = a["L0_ffn_b3"].reshape(UNITS, 2 * BOT).T

    c = np.zeros((P, NC_), np.float32)

    def put(i, v):
        c[:, C_AT[i]:C_AT[i + 1]] = v
    p = np.arange(P)
    put(C_ID, p[:, None] == p[None, :])
    put(C_TRI, p[:, None] < p[None, :])
    put(C_CAUS, np.where(np.arange(SEQ)[None, :] > (p % SEQ)[:, None], -1e30, 0.0))
    inv = (1.0 / 10000.0 ** (np.arange(0, HD, 2, dtype=np.float32) / np.float32(HD))).astype(np.float32)
    ang = (p % SEQ).astype(np.float32)[:, None] * inv[None, :]
    cos, sin = np.cos(ang), np.sin(ang)
    scale = 1.0 / np.sqrt(np.float32(HD))
    cos2, sin2 = np.concatenate([cos, cos], 1), np.concatenate([-sin, sin], 1)
    put(C_COS, np.concatenate([cos2 * scale, cos2], 1))
    put(C_SIN, np.concatenate([sin2 * scale, sin2], 1))
    put(C_M0, (p // HD)[:, None] == np.arange(H0)[None, :])
    put(C_M1, (p // HD)[:, None] == np.arange(H1)[None, :])
    put(C_IOTA, np.arange(P)[None, :])
    put(C_PAIR, np.arange(UNITS)[None, :])

    biases = np.concatenate([b12.reshape(P, -1), b3], 1)
    arrays = {"xp": x, "wt": wt, "proj": proj, "rows": a["L0_tok_b"], "consts": c, "experts": experts, "biases": biases,
              "bl": a["L0_ffn_bl"]}
    arrays = {f"in_{k}": np.ascontiguousarray(v) for k, v in arrays.items()}
    nc = bacc.Bacc("TRN2", target_bir_lowering=False, num_devices=1)
    args = [nc.dram_tensor(k, v.shape, F32, kind="ExternalInput").ap() for k, v in arrays.items()]
    out = nc.dram_tensor("out", (TOKENS, D), F32, kind="ExternalOutput").ap()
    vit_layer(nc, *args, out)
    r = run_bass_kernel_spmd(nc, [arrays], core_ids=[0])
    return r.results[0]["out"].reshape(TILES * 2, SEQ, D)
```
